# Optimizing a Trainium2 kernel written in Bass

```python
import numpy as np
import jax
import jax.numpy as jnp

def _softmax(x, axis=-1):
    return jax.nn.softmax(x, axis=axis)

def _gelu(x):
    return jax.nn.gelu(x, approximate=True)

def _silu(x):
    return jax.nn.silu(x)

def _sigmoid(x):
    return jax.nn.sigmoid(x)

def _layernorm(x, axis=-1, eps=1e-05):
    m = jnp.mean(x, axis=axis, keepdims=True)
    v = jnp.var(x, axis=axis, keepdims=True)
    return (x - m) / jnp.sqrt(v + eps)

def _scatter_add(tgt, idx, src, axis=0):
    return tgt.at[idx].add(src)

def _segment_sum(src, seg, n):
    return jax.ops.segment_sum(src, seg, n)
kernel_name = 'mk_gnn_resnorm_d2_gnn_r64_878830'

def setup_inputs(seed: int=0):
    np.random.seed(seed)
    _w = jnp.asarray

    def _rec_inputs():
        import jax
        import jax.numpy as jnp
        _gk = jax.random.key(seed)
        x = -0.000202 + 1 * jax.random.normal(jax.random.fold_in(_gk, 1), (100000, 64), jnp.float32)
        src = jax.random.randint(jax.random.fold_in(_gk, 2), (25000,), 0, 100000, jnp.int32)
        dst = jnp.minimum((100000 * jax.random.uniform(jax.random.fold_in(_gk, 3), (25000,)) ** 2.0).astype(jnp.int32), 99999)
        _o = jnp.argsort(dst, stable=True)
        src = src[_o]
        dst = dst[_o]
        edge_type_16 = jax.random.randint(jax.random.fold_in(_gk, 13), (25000,), 0, 16, jnp.int32)
        edge_type_5 = jax.random.randint(jax.random.fold_in(_gk, 14), (25000,), 0, 5, jnp.int32)
        return (x, src, dst, edge_type_16, edge_type_5)
    x, src, dst, edge_type_16, edge_type_5 = _rec_inputs()

    def _L0_gnn_setup():
        import jax, jax.numpy as jnp
        import numpy as np
        N = 100000
        E = 25000
        D = 64
        R = 5
        L = 10
        LN_EPS = 1e-05
        key = jax.random.key(seed)
        ks = jax.random.split(key, 8)
        annotation_feature = jax.random.normal(ks[0], (N, D), dtype=jnp.float32)
        annotation_edges = jax.random.randint(ks[1], (2, E), 0, N)
        annotation_edges_type = jax.random.randint(ks[2], (E,), 0, R)
        scale = 0.05
        W_rel = jax.random.normal(ks[3], (L, R, D, D), dtype=jnp.float32) * scale
        W_root = jax.random.normal(ks[4], (L, D, D), dtype=jnp.float32) * scale
        bias = jnp.zeros((L, D), dtype=jnp.float32)
        ln_gamma = jnp.ones((L, D), dtype=jnp.float32)
        ln_beta = jnp.zeros((L, D), dtype=jnp.float32)
        return {'annotation_feature': annotation_feature, 'annotation_edges': annotation_edges, 'annotation_edges_type': annotation_edges_type, 'W_rel': W_rel, 'W_root': W_root, 'bias': bias, 'ln_gamma': ln_gamma, 'ln_beta': ln_beta}
    _L0_gnn_all = _L0_gnn_setup()
    _L0_gnn_in = {k: v for k, v in _L0_gnn_all.items() if k in ('W_rel', 'W_root', 'bias', 'ln_gamma', 'ln_beta')}
    del _L0_gnn_all

    def _L1_gnn_setup():
        import jax, jax.numpy as jnp
        import numpy as np
        N_NODES = 3125
        N_EDGES = 31250
        NUM_RELS = 16
        F_IN = 64
        F_OUT = 64
        key = jax.random.key(seed)
        k0, k1, k2, k3, k4 = jax.random.split(key, 5)
        feat = jax.random.normal(k0, (N_NODES, F_IN), dtype=jnp.float32)
        W = jax.random.normal(k1, (NUM_RELS, F_OUT, F_IN), dtype=jnp.float32) * 0.05
        src = jax.random.randint(k2, (N_EDGES,), 0, N_NODES, dtype=jnp.int32)
        dst = jax.random.randint(k3, (N_EDGES,), 0, N_NODES, dtype=jnp.int32)
        etype = jax.random.randint(k4, (N_EDGES,), 0, NUM_RELS, dtype=jnp.int32)
        return {'feat': feat, 'W': W, 'src': src, 'dst': dst, 'etype': etype}
    _L1_gnn_all = _L1_gnn_setup()
    _L1_gnn_in = {k: v for k, v in _L1_gnn_all.items() if k in ('W',)}
    del _L1_gnn_all
    return {'x': x, 'src': src, 'dst': dst, 'edge_type_16': edge_type_16, 'edge_type_5': edge_type_5, 'L0_gnn_W_rel': _L0_gnn_in['W_rel'], 'L0_gnn_W_root': _L0_gnn_in['W_root'], 'L0_gnn_bias': _L0_gnn_in['bias'], 'L0_gnn_ln_gamma': _L0_gnn_in['ln_gamma'], 'L0_gnn_ln_beta': _L0_gnn_in['ln_beta'], 'L1_gnn_W': _L1_gnn_in['W']}

def reference(x, src, dst, edge_type_16, edge_type_5, L0_gnn_W_rel, L0_gnn_W_root, L0_gnn_bias, L0_gnn_ln_gamma, L0_gnn_ln_beta, L1_gnn_W):
    import jax
    import jax.numpy as jnp

    def _L0_gnn_ref(annotation_feature, annotation_edges, annotation_edges_type, W_rel, W_root, bias, ln_gamma, ln_beta):
        import jax, jax.numpy as jnp
        import numpy as np
        N = 100000
        E = 25000
        D = 64
        R = 5
        L = 10
        LN_EPS = 1e-05
        src = annotation_edges[0]
        dst = annotation_edges[1]
        n_nodes = annotation_feature.shape[0]

        def layer(x, params):
            Wr, Wo, b, g, be = params
            h = jnp.einsum('nd,rdk->rnk', x, Wr)
            msg = h[annotation_edges_type, src]
            agg = jax.ops.segment_sum(msg, dst, num_segments=n_nodes)
            out = jax.nn.relu(agg + x @ Wo + b)
            y = out + x
            mu = jnp.mean(y, axis=-1, keepdims=True)
            var = jnp.mean(jnp.square(y - mu), axis=-1, keepdims=True)
            y = (y - mu) * jax.lax.rsqrt(var + LN_EPS) * g + be
            return (y, None)
        y, _ = jax.lax.scan(layer, annotation_feature, (W_rel, W_root, bias, ln_gamma, ln_beta))
        return y

    def _L1_gnn_ref(feat, W, src, dst, etype):
        import jax, jax.numpy as jnp
        import numpy as np
        N_NODES = 3125
        N_EDGES = 31250
        NUM_RELS = 16
        F_IN = 64
        F_OUT = 64
        n_dst = feat.shape[0]
        xw = jnp.einsum('rof,nf->rno', W, feat)
        msg = xw[etype, src]
        return jax.ops.segment_sum(msg, dst, num_segments=n_dst)
    edge_index = jnp.stack([src, dst])
    x = _layernorm(x + _L0_gnn_ref(x, edge_index, edge_type_5, L0_gnn_W_rel, L0_gnn_W_root, L0_gnn_bias, L0_gnn_ln_gamma, L0_gnn_ln_beta), axis=-1)
    x = _layernorm(x + _L1_gnn_ref(x, L1_gnn_W, src, dst, edge_type_16), axis=-1)
    return x

_drawn_inputs = setup_inputs


def setup_inputs(seed=0):
    import zlib

    import numpy as np

    out = dict(_drawn_inputs(seed))
    spreads = {'L0_gnn_bias': (0.0, 0.1), 'L0_gnn_ln_gamma': (1.0, 0.2), 'L0_gnn_ln_beta': (0.0, 0.1)}
    factors = {}
    for name, (base, spread) in spreads.items():
        noise = np.random.default_rng([zlib.crc32(name.encode()), seed]).standard_normal(out[name].shape)
        drawn = base * np.exp(spread * noise) if base else spread * noise
        out[name] = jnp.asarray(drawn.astype(out[name].dtype))
    for name, factor in factors.items():
        out[name] = (out[name] * factor).astype(out[name].dtype)
    return out
```

```python
from contextlib import ExitStack

import numpy as np

import concourse.bass as bass
from concourse import mybir

F32 = mybir.dt.float32
I32 = mybir.dt.int32
U32 = mybir.dt.uint32
U8 = mybir.dt.uint8
ALU = mybir.AluOpType
ACT = mybir.ActivationFunctionType

NODES, EDGES, D, LAYERS, RELS, RELS1 = 100000, 25000, 64, 10, 5, 16
EPS = 1e-5
P = 125
CH = 8
ROWS = P * CH
PAIRS = CH // 2
COLS = PAIRS * P
TILES = NODES // ROWS
ETILES = EDGES // ROWS
CHUNKS = EDGES // P
Q = CHUNKS // 2
GROUP = 5
GROUPS_A_TURN = TILES // GROUP // LAYERS
TABLE = EDGES + 1
NOWHERE = float(1 << 20)

LOAD, LAYER, SKIP, LAST, ADD, OUT = "load", "layer", "skip", "last", "add", "out"


class Step:

    def __init__(self, kind, tile, x, w=None, vec=None, rows=None, agg=None, other=None, layer=0):
        self.kind, self.tile, self.x, self.w, self.vec = kind, tile, x, w, vec
        self.rows, self.agg, self.other, self.layer = rows, agg, other, layer
        self.p = self.n = self.a = self.before = None


def number(steps):
    p = n = a = 0
    last = {}
    for s in steps:
        s.before = last.get(s.tile)
        if s.kind != ADD and not (s.kind == LAST and s.rows is None):
            s.p = p
            p += 1
            last[s.tile] = ("first", p)
        if s.kind == ADD:
            s.a = a
            a += 1
        if s.kind not in (LOAD, OUT):
            s.n = n
            n += 1
            last[s.tile] = ("norm", n)
    return steps


def build(nc, x, src, dst, type16, type5, w_rel, w_root, bias, gamma, beta, w1, places, out):
    sums_now = nc.dram_tensor("message_sums_now", [TABLE, D], F32, kind="Internal").ap()
    table = nc.dram_tensor("message_sums_of_layers", [(LAYERS + 1) * EDGES, D], F32, kind="Internal").ap()
    owner_of = nc.dram_tensor("owner_of_node", [NODES, 1], I32, kind="Internal").ap()
    source_rows = nc.dram_tensor("source_rows", [128, ETILES * COLS], F32, kind="Internal").ap()

    with ExitStack() as ctx:
        def sb(name, shape, dt=F32):
            return ctx.enter_context(nc.sbuf_tensor(name, shape, dt))

        def sem(name):
            return ctx.enter_context(nc.semaphore(name))

        bank = [ctx.enter_context(nc.psum_tensor(f"bank{i}", [128, 512], F32)) for i in range(8)]
        source = sb("source", [128, ETILES * COLS])
        gathered = sb("gathered", [128, CHUNKS * D])
        same = sb("same", [P, CHUNKS * P], U8)
        kind8 = sb("kind8", [128, ETILES * COLS], U8)
        rows = sb("rows", [128, 2 * GROUP * CH * D])
        work = sb("work", [128, 6600])
        w_all = sb("w_all", [128, LAYERS, 128])
        w_now = sb("w_now", [128, 128])
        rel_now = sb("rel_now", [128, RELS, 128])
        ident = sb("ident", [128, 128])
        center = sb("center", [128, 128])
        mean = sb("mean", [128, 128])
        vec = sb("vec", [128, LAYERS, 4])
        vec_now = sb("vec_now", [128, 4])
        eps = sb("eps", [128, 1])
        follows = sb("follows", [Q, 2, 2, Q])
        first_sum = sb("first_sum", [Q, 2, D])
        last_sum = sb("last_sum", [Q, 2, D])
        owner = sb("owner", [P, CHUNKS], U32)
        target = sb("target", [P, CHUNKS], U32)
        goal = sb("goal", [P, CHUNKS], U32)
        target_now = sb("target_now", [P, GROUP * CH], U32)
        goal_now = sb("goal_now", [P, GROUP * CH], U32)
        last_owner = sb("last_owner", [Q, 2])
        last_owner_row = sb("last_owner_row", [Q, 2], U32)
        last_owner_now = sb("last_owner_now", [Q, 2], U32)
        base = sb("base", [128, 1])

        x_buf = [work[:, i * COLS:(i + 1) * COLS] for i in range(GROUP)]
        sq_buf = [work[:, (GROUP + i) * COLS:(GROUP + 1 + i) * COLS] for i in range(2)]
        rstd_buf = [work[:, (GROUP + 2 + i) * COLS:(GROUP + 3 + i) * COLS] for i in range(2)]
        picked = [work[:, i * COLS:(i + 1) * COLS] for i in range(3)]
        sent = [work[:, (3 + i) * COLS:(4 + i) * COLS] for i in range(2)]
        sent_rows = [work[0:P, 2500 + i * 512:3012 + i * 512] for i in range(2)]
        same_f = [work[0:P, 3524 + i * 1000:4524 + i * 1000] for i in range(2)]
        sums = [work[0:P, 5524 + i * 512:6036 + i * 512] for i in range(2)]

        def tile_rows(k):
            return rows[0:P, k * CH * D:(k + 1) * CH * D]

        def gathered_rows(t):
            return gathered[0:P, t * CH * D:(t + 1) * CH * D]

        def source_tile(t):
            return source[:, t * COLS:(t + 1) * COLS]

        names = ("rows_in p first add q square v ln rstd z norm stored corr_in corr_got corr corr_sum "
                 "corr_put gathers now now2 rel picked sent sent_rows same_f sums mm turned summed "
                 "store0 store1 agg0 agg1 agg2 agg3 agg4 agg5 put owners_put owners_got targets_in sources_in passed").split()
        s = {n: sem("s_" + n) for n in names}
        kept = "corr_got corr_put gathers put owners_put owners_got targets_in sources_in".split()

        def stream_tensor(pe, steps, hook=None, agg_ready=None):
            def turn(s_, rows_ap, dest):
                for j in range(PAIRS):
                    last = pe.transpose(dest[:, j * P:(j + 1) * P], rows_ap[:, 2 * j * D:(2 * j + 2) * D],
                                        ident[0:P, 0:P])
                return last

            for i in range(len(steps) + 2):
                if hook and i == 8:
                    hook()
                if i < len(steps) and steps[i].p is not None:
                    st = steps[i]
                    if st.p >= 2:
                        pe.wait_ge(s["first"], st.p - 1)
                    if st.before and st.kind in (LAYER, OUT):
                        pe.wait_ge(s[st.before[0]], st.before[1])
                    dest = bank[st.p % 2]
                    if agg_ready:
                        agg_ready(pe, st)
                    if st.kind in (LOAD, SKIP, LAST):
                        last = turn(st, st.rows, dest)
                    elif st.kind == OUT:
                        for j in range(PAIRS):
                            last = pe.transpose(dest[0:P, j * 128:(j + 1) * 128], st.x[:, j * P:(j + 1) * P],
                                                ident[:, :])
                    else:
                        last = pe.matmul(dest[:, 0:COLS], st.w, st.x, start=True, stop=st.agg is None,
                                         skip_group_check=True)
                        if st.agg is not None:
                            for j in range(PAIRS):
                                last = pe.matmul(dest[:, j * P:(j + 1) * P], st.agg[:, 2 * j * D:(2 * j + 2) * D],
                                                 ident[0:P, 0:P], start=False, stop=True, skip_group_check=True)
                    last.then_inc(s["p"], 1)
                if 1 <= i <= len(steps) and steps[i - 1].n is not None:
                    st = steps[i - 1]
                    if st.n >= 3:
                        pe.wait_ge(s["norm"], st.n - 2)
                    if st.kind == ADD:
                        pe.wait_ge(s["add"], st.a + 1)
                    elif st.p is not None:
                        pe.wait_ge(s["first"], st.p + 1)
                    elif st.before:
                        pe.wait_ge(s[st.before[0]], st.before[1])
                    pe.matmul(bank[2 + st.n % 3][:, 0:COLS], center[:, :], st.x, start=True,
                              stop=True).then_inc(s["q"], 1)
                if i >= 2 and steps[i - 2].n is not None:
                    st = steps[i - 2]
                    pe.wait_ge(s["square"], st.n + 1)
                    if st.n >= 2:
                        pe.wait_ge(s["ln"], st.n - 1)
                    pe.matmul(bank[5 + st.n % 2][:, 0:COLS], mean[:, :], sq_buf[st.n % 2], start=True,
                              stop=True).then_inc(s["v"], 1)

        def stream_scalar(act, steps):
            act.preload_act_table_set("natural_log_exp_and_others")
            for i in range(len(steps) + 1):
                if i < len(steps) and steps[i].n is not None:
                    st = steps[i]
                    act.wait_ge(s["q"], st.n + 1)
                    if st.n >= 2:
                        act.wait_ge(s["v"], st.n - 1)
                    act.activation(sq_buf[st.n % 2], bank[2 + st.n % 3][:, 0:COLS], ACT.Square,
                                   bias=st.vec[:, 1:2] if st.kind == LAYER else 0.0).then_inc(s["square"], 1)
                if i >= 1 and steps[i - 1].n is not None:
                    k = steps[i - 1].n
                    act.wait_ge(s["v"], k + 1)
                    if k >= 2:
                        act.wait_ge(s["norm"], k - 1)
                    act.activation(rstd_buf[k % 2], bank[5 + k % 2][:, 0:COLS], ACT.Ln,
                                   bias=eps[:, 0:1]).then_inc(s["ln"], 1)
                    act.wait_ge(s["ln"], k + 1)
                    act.activation(rstd_buf[k % 2], rstd_buf[k % 2], ACT.Exp, scale=-0.5).then_inc(s["rstd"], 1)

        def stream_vector(dve, steps, hook=None):
            for i in range(len(steps) + 3):
                if hook and i == 10:
                    hook()
                if i < len(steps):
                    st = steps[i]
                    if st.p is not None:
                        dve.wait_ge(s["p"], st.p + 1)
                        pr = bank[st.p % 2]
                        if st.kind == LOAD:
                            done = dve.tensor_copy(st.x, pr[:, 0:COLS])
                        elif st.kind == OUT:
                            done = dve.tensor_copy(st.rows, pr[0:P, 0:CH * D])
                        elif st.kind == LAYER:
                            done = dve.scalar_tensor_tensor(out=st.x, in0=pr[:, 0:COLS], scalar=st.vec[:, 0:1],
                                                            in1=st.x, op0=ALU.max, op1=ALU.add)
                        else:
                            if st.before:
                                dve.wait_ge(s[st.before[0]], st.before[1])
                            done = dve.tensor_tensor(st.x, pr[:, 0:COLS], st.x, ALU.add)
                        done.then_inc(s["first"], 1)
                    elif st.kind == ADD:
                        dve.tensor_tensor(st.x, st.x, st.other, ALU.add).then_inc(s["add"], 1)
                if i >= 3 and steps[i - 3].n is not None:
                    st = steps[i - 3]
                    centered, rstd = bank[2 + st.n % 3][:, 0:COLS], rstd_buf[st.n % 2]
                    dve.wait_ge(s["rstd"], st.n + 1)
                    if st.kind == LAYER:
                        dve.scalar_tensor_tensor(out=st.x, in0=centered, scalar=st.vec[:, 1:2], in1=rstd,
                                                 op0=ALU.add, op1=ALU.mult).then_inc(s["z"], 1)
                        st_z = sum(1 for o in steps[:i - 2] if o.kind == LAYER)
                        dve.wait_ge(s["z"], st_z)
                        dve.tensor_scalar(st.x, st.x, st.vec[:, 2:3], st.vec[:, 3:4], ALU.mult,
                                          ALU.add).then_inc(s["norm"], 1)
                    else:
                        dve.tensor_tensor(st.x, centered, rstd, ALU.mult).then_inc(s["norm"], 1)

        def message_engines(block, rels, rel_tile, table_rows, before_sync, before_vector):
            @block.sync
            def _(sp):
                before_sync(sp)
                for t in range(ETILES):
                    sp.wait_ge(s["summed"], t + 1)
                    now = sums_now[t * ROWS:(t + 1) * ROWS, :].rearrange("(p c) d -> p (c d)", c=CH)
                    sp.dma_start(table_rows(t), sums[t % 2]).then_inc(s[f"store{t % 2}"], 16)
                    sp.dma_start(now, sums[t % 2]).then_inc(s[f"store{t % 2}"], 16)
                sp.wait_ge(s["store0"], 32 * ((ETILES + 1) // 2))
                sp.wait_ge(s["store1"], 32 * (ETILES // 2))

            @block.gpsimd
            def _(pool):
                for t in range(ETILES):
                    if t >= 2:
                        pool.wait_ge(s["sums"], t - 1)
                    pool.tensor_copy(same_f[t % 2], same[:, t * CH * P:(t + 1) * CH * P]).then_inc(s["same_f"], 1)

            @block.vector
            def _(dve):
                before_vector(dve)
                for t in range(ETILES):
                    for r in range(rels):
                        k = t * rels + r
                        if k >= 3:
                            dve.wait_ge(s["mm"], k - 2)
                        dve.scalar_tensor_tensor(out=picked[k % 3], in0=kind8[:, t * COLS:(t + 1) * COLS],
                                                 scalar=float(r), in1=source_tile(t), op0=ALU.is_equal,
                                                 op1=ALU.mult).then_inc(s["picked"], 1)

            @block.tensor
            def _(pe):
                pe.wait_ge(s["rel"], 32)
                for i in range(ETILES + 2):
                    if i < ETILES:
                        if i >= 2:
                            pe.wait_ge(s["sent"], i - 1)
                        for r in range(rels):
                            k = i * rels + r
                            pe.wait_ge(s["picked"], k + 1)
                            pe.matmul(bank[i % 2][:, 0:COLS], rel_tile(r), picked[k % 3], start=(r == 0),
                                      stop=(r == rels - 1)).then_inc(s["mm"], 1)
                    if 1 <= i <= ETILES:
                        t = i - 1
                        pe.wait_ge(s["sent"], t + 1)
                        if t >= 2:
                            pe.wait_ge(s["sent_rows"], t - 1)
                        for j in range(PAIRS):
                            last = pe.transpose(bank[2 + t % 2][0:P, j * 128:(j + 1) * 128],
                                                sent[t % 2][:, j * P:(j + 1) * P], ident[:, :])
                        last.then_inc(s["turned"], 1)
                    if i >= 2:
                        t = i - 2
                        pe.wait_ge(s["sent_rows"], t + 1)
                        pe.wait_ge(s["same_f"], t + 1)
                        if t >= 2:
                            pe.wait_ge(s["summed"], t - 1)
                        for c in range(CH):
                            last = pe.matmul(bank[4 + t % 2][0:P, c * D:(c + 1) * D],
                                             same_f[t % 2][:, c * P:(c + 1) * P],
                                             sent_rows[t % 2][:, c * D:(c + 1) * D], start=True, stop=True,
                                             skip_group_check=True)
                        last.then_inc(s["sums"], 1)

            @block.scalar
            def _(act):
                for i in range(ETILES + 2):
                    if i < ETILES:
                        act.wait_ge(s["mm"], rels * (i + 1))
                        if i >= 2:
                            act.wait_ge(s["turned"], i - 1)
                        act.activation(sent[i % 2], bank[i % 2][:, 0:COLS], ACT.Copy).then_inc(s["sent"], 1)
                    if 1 <= i <= ETILES:
                        t = i - 1
                        act.wait_ge(s["turned"], t + 1)
                        if t >= 2:
                            act.wait_ge(s["sums"], t - 1)
                        act.activation(sent_rows[t % 2], bank[2 + t % 2][0:P, :], ACT.Copy).then_inc(s["sent_rows"], 1)
                    if i >= 2:
                        t = i - 2
                        act.wait_ge(s["sums"], t + 1)
                        if t >= 2:
                            act.wait_ge(s[f"store{t % 2}"], 32 * (t // 2))
                        act.activation(sums[t % 2], bank[4 + t % 2][0:P, :], ACT.Copy).then_inc(s["summed"], 1)

        def runs_on_sync(sp):
            for c in range(CH):
                q0 = (c % 4) * ETILES
                sp.dma_start(first_sum[q0:q0 + ETILES, c // 4, :],
                             sums_now[0:EDGES, :].rearrange("(t q) d -> t q d", q=ROWS)[:, c, :]
                             ).then_inc(s["corr_in"], 16)

        def runs_on_gather(pool):
            for h in range(2):
                pool.indirect_dma_start(last_sum[:, h, :], None, sums_now,
                                        bass.IndirectOffsetOnAxis(ap=last_owner_row[:, h:h + 1], axis=0)
                                        ).then_inc(s["corr_got"], 16)

        def runs_on_tensor(pe):
            pe.wait_ge(s["corr_in"], 16 * CH)
            for h in range(2):
                for k in range(2):
                    last = pe.matmul(bank[7][0:Q, h * D:(h + 1) * D], follows[:, k, h, :], first_sum[:, k, :],
                                     start=(h == 0 and k == 0), stop=(h == 1 and k == 1), skip_group_check=True)
            last.then_inc(s["corr"], 1)

        def runs_on_vector(dve, layer):
            dve.wait_ge(s["corr"], 1)
            dve.wait_ge(s["corr_got"], layer * 32 + 32)
            dve.tensor_tensor(last_sum[:, :, :].rearrange("q h d -> q (h d)"), bank[7][0:Q, 0:2 * D],
                              last_sum[:, :, :].rearrange("q h d -> q (h d)"), ALU.add).then_inc(s["corr_sum"], 1)

        def runs_on_scatter(pool, layer):
            pool.wait_ge(s["corr_sum"], 1)
            for to, at in ((sums_now, last_owner_row), (table, last_owner_now)):
                for h in range(2):
                    pool.indirect_dma_start(to, bass.IndirectOffsetOnAxis(ap=at[:, h:h + 1], axis=0),
                                            last_sum[:, h, :], None).then_inc(s["corr_put"], 16)
            pool.wait_ge(s["corr_put"], layer * 64 + 64)
            pool.sem_inc(s["passed"], 1)

        def indices_now(dve):
            dve.tensor_scalar(base[:, :], base[:, :], float(EDGES), None, ALU.add).then_inc(s["now"], 1)
            dve.wait_ge(s["now"], 1)
            dve.tensor_scalar(last_owner_now[:, :], last_owner[:, :], base[0:Q, :], None, ALU.add).then_inc(s["now"], 1)

        def finish_turn():
            nc.all_engine_barrier()
            for n in names:
                if n not in kept:
                    nc.gpsimd.sem_clear(s[n])
            nc.all_engine_barrier()

        def small(a, b, n=Q, dt=F32):
            v = work[0:n, a:b]
            return v if dt is F32 else v.bitcast(dt)

        half_chunks = 2 * P
        dst_i, prev_i, src_i = (small(k * half_chunks, (k + 1) * half_chunks, dt=I32) for k in range(3))
        dst_f, prev_f, src_f, own, goal_f, scratch = (small(k * half_chunks, (k + 1) * half_chunks) for k in range(3, 9))
        count = small(2250, 2252)
        last_diag, place_diag = small(2300, 2300 + 2 * Q), small(2500, 2500 + 2 * Q)
        ones = small(2700, 2700 + Q)
        after = small(2800, 2800 + 4 * Q)
        place = small(3200, 3204)
        no_owner = small(3300, 4100, P, I32)
        edge_row = small(4100, 4100 + CHUNKS, P, I32)
        dst_col = small(4300, 4300 + CHUNKS, P)
        zero_row = small(4500, 4500 + D, 1)
        bias_cols = small(4600, 4600 + LAYERS, 128)
        src_col = small(4700, 4700 + CHUNKS, P, U32)
        owner_i = small(4900, 4900 + CHUNKS, P, I32)

        def by_chunk(tile_, k):
            return tile_.rearrange("p (t c) -> p c t", c=CH)[:, 4 * k:4 * k + 4, :]

        with nc.Block() as block:
            @block.sync
            def _(sp):
                n = 0
                dst_t, src_t = (a.rearrange("(t q) -> t q", q=ROWS) for a in (dst, src))
                for c in range(CH):
                    q0, k0 = (c % 4) * ETILES, (c // 4) * P
                    sp.dma_start(dst_i[q0:q0 + ETILES, k0:k0 + P], dst_t[:, c * P:(c + 1) * P]).then_inc(s["rows_in"], 16)
                    sp.dma_start(src_i[q0:q0 + ETILES, k0:k0 + P], src_t[:, c * P:(c + 1) * P]).then_inc(s["rows_in"], 16)
                    if c:
                        sp.dma_start(prev_i[q0:q0 + ETILES, k0:k0 + P],
                                     dst_t[:, c * P - 1:(c + 1) * P - 1]).then_inc(s["rows_in"], 16)
                    n += 3 if c else 2
                sp.dma_start(prev_i[1:ETILES, 0:P], dst[ROWS - 1:EDGES - 1].rearrange("(t q) -> t q", q=ROWS)[:, 0:P]
                             ).then_inc(s["rows_in"], 16)
                sp.dma_start(prev_i[0:1, 1:P], dst[0:P - 1].rearrange("(a n) -> a n", a=1)).then_inc(s["rows_in"], 16)
                sp.dma_start(place, places).then_inc(s["rows_in"], 16)
                assert n + 3 == 26
                sp.wait_ge(s["same_f"], 5)
                for half in range(2):
                    part = slice(64 * half, 64 * half + 64)
                    sp.dma_start(w_all[part, :, part], w_root.rearrange("l d k -> d l k")).then_inc(s["rel"], 16)
                    for dest, a in ((bias_cols[part, :], bias), (vec[part, :, 2], gamma), (vec[part, :, 3], beta)):
                        sp.dma_start(dest, a.rearrange("l d -> d l"), allow_slow_non_contiguous=True).then_inc(s["rel"], 16)
                sp.dma_start(owner_of.rearrange("(p n) o -> p (n o)", p=P), no_owner).then_inc(s["stored"], 16)
                sp.dma_start(sums_now[EDGES:TABLE, :], zero_row).then_inc(s["stored"], 16)
                sp.wait_ge(s["stored"], 32)

            @block.gpsimd
            def _(pool):
                for a in (w_all[:, :, :], rel_now[:, :, :], center[:, :], mean[:, :], ident[:, :]):
                    last = pool.memset(a, 0.0)
                last.then_inc(s["picked"], 1)
                pool.wait_ge(s["picked"], 1)
                for half in range(2):
                    part = slice(64 * half, 64 * half + 64)
                    pool.memset(center[part, part], -1.0 / D)
                    pool.memset(mean[part, part], 1.0 / D).then_inc(s["picked"], 1)
                pool.wait_ge(s["picked"], 3)
                for a, v in ((ident[:, :], 1.0), (center[:, :], 1.0 - 1.0 / D)):
                    pool.affine_select(out=a, in_=a, compare_op=ALU.not_equal, fill=v, base=0,
                                       pattern=[[-1, 128]], channel_multiplier=1).then_inc(s["same_f"], 1)
                pool.memset(eps[:, :], EPS)
                pool.memset(base[:, :], -float(EDGES))
                pool.memset(ones, 1.0).then_inc(s["same_f"], 1)
                pool.memset(no_owner, EDGES).then_inc(s["same_f"], 1)
                pool.iota(edge_row, pattern=[[ROWS, ETILES], [1, CH]], base=0, channel_multiplier=CH)
                pool.memset(zero_row, 0.0).then_inc(s["same_f"], 1)

            @block.vector
            def _(dve):
                done = [0]

                def then(ins):
                    done[0] += 1
                    ins.then_inc(s["z"], 1)
                    dve.wait_ge(s["z"], done[0])

                dve.wait_ge(s["rows_in"], 16 * 26)
                dve.memset(prev_i[0:1, 0:1], -1).then_inc(s["now"], 1)
                dve.wait_ge(s["now"], 1)
                dve.tensor_copy(dst_f, dst_i)
                dve.tensor_copy(src_f, src_i)
                then(dve.tensor_copy(prev_f, prev_i))
                then(dve.tensor_tensor(own, dst_f, prev_f, ALU.not_equal))
                then(dve.tensor_scalar(own, own, -NOWHERE, NOWHERE, ALU.mult, ALU.add))
                then(dve.tensor_tensor(goal_f, own, dst_f, ALU.add))
                for h in range(2):
                    then(dve.tensor_scalar(scratch[:, 0:P], dst_f[:, h * P:(h + 1) * P],
                                           dst_f[:, (h + 1) * P - 1:(h + 1) * P], None, ALU.is_equal, ALU.add,
                                           accum_out=count[:, h:h + 1]))
                then(dve.tensor_scalar(count, count, -float(CH), None, ALU.mult))
                dve.tensor_tensor(last_owner_row[:, :], count, place[:, 2:4], ALU.add)
                then(dve.tensor_tensor(last_owner[:, :], count, place[:, 2:4], ALU.add))
                dve.wait_ge(s["same_f"], 3)
                for h in range(2):
                    dve.tensor_scalar(last_diag[:, h * Q:(h + 1) * Q], ident[0:Q, 0:Q],
                                      dst_f[:, (h + 1) * P - 1:(h + 1) * P], None, ALU.mult)
                    then(dve.tensor_scalar(place_diag[:, h * Q:(h + 1) * Q], ident[0:Q, 0:Q], place[:, h:h + 1],
                                           None, ALU.mult))
                done_before_products = done[0]
                assert done_before_products == 10
                dve.wait_ge(s["p"], 1)
                for k in range(2):
                    psum = [bank[b][0:P, k * Q:(k + 1) * Q].rearrange("p (c t) -> p c t", c=4) for b in range(3)]
                    dve.tensor_copy(by_chunk(dst_col, k), psum[0])
                    dve.tensor_copy(by_chunk(target[:, :], k), psum[0])
                    dve.tensor_copy(by_chunk(goal[:, :], k), psum[1])
                    dve.tensor_copy(by_chunk(src_col, k), psum[2])
                for k in range(2):
                    for h in range(2):
                        a = after[:, (2 * k + h) * Q:(2 * k + h + 1) * Q]
                        then(dve.tensor_scalar(a, bank[4][0:Q, h * Q:(h + 1) * Q], place[:, k:k + 1], None, ALU.is_lt))
                        then(dve.scalar_tensor_tensor(out=follows[:, k, h, :], in0=bank[3][0:Q, h * Q:(h + 1) * Q],
                                                      scalar=dst_f[:, k * P:k * P + 1], in1=a, op0=ALU.is_equal,
                                                      op1=ALU.mult))
                dve.wait_ge(s["rel"], 16 * 8)
                dve.tensor_scalar(vec[:, :, 0], bias_cols, -1.0, None, ALU.mult)
                then(dve.tensor_copy(vec[:, :, 1], bank[5][:, 0:LAYERS]))

            @block.tensor
            def _(pe):
                pe.wait_ge(s["z"], 10)
                for k in range(2):
                    for b, a in enumerate((dst_f, goal_f, src_f)):
                        pe.transpose(bank[b][0:P, k * Q:(k + 1) * Q], a[:, k * P:(k + 1) * P], ident[0:Q, 0:Q])
                pe.matmul(bank[3][0:Q, 0:2 * Q], ones, last_diag, start=True, stop=True)
                pe.matmul(bank[4][0:Q, 0:2 * Q], ones, place_diag, start=True, stop=True)
                pe.wait_ge(s["rel"], 16 * 8)
                pe.matmul(bank[5][:, 0:LAYERS], center[:, :], bias_cols, start=True, stop=True).then_inc(s["p"], 1)
        finish_turn()

        with nc.Block() as block:
            dst_here = [rows[0:P, i * ROWS:(i + 1) * ROWS].bitcast(I32) for i in range(2)]

            @block.sync
            def _(sp):
                for t in range(ETILES):
                    if t >= 2:
                        sp.wait_ge(s["same_f"], t - 1)
                    sp.dma_start(dst_here[t % 2], dst[t * ROWS:(t + 1) * ROWS].partition_broadcast(P)
                                 ).then_inc(s[f"agg{t % 2}"], 16)
                sp.wait_ge(s["first"], ETILES)
                sp.dma_start(source_rows, source[:, :]).then_inc(s["stored"], 16)
                sp.wait_ge(s["stored"], 16)

            @block.vector
            def _(dve):
                for t in range(ETILES):
                    dve.wait_ge(s[f"agg{t % 2}"], 16 * (t // 2 + 1))
                    for c in range(CH):
                        k = t * CH + c
                        last = dve.tensor_scalar(same[:, k * P:(k + 1) * P], dst_here[t % 2][:, c * P:(c + 1) * P],
                                                 dst_col[:, k:k + 1], None, ALU.is_equal)
                    last.then_inc(s["same_f"], 1)
                dve.wait_ge(s["owners_got"], 16 * CHUNKS)
                dve.tensor_copy(owner[:, :], owner_i)

            @block.gpsimd
            def _(pool):
                for c in range(CHUNKS):
                    pool.indirect_dma_start(gathered[0:P, c * D:(c + 1) * D], None, x,
                                            bass.IndirectOffsetOnAxis(ap=src_col[:, c:c + 1], axis=0)
                                            ).then_inc(s["sources_in"], 16)
                for c in range(CHUNKS):
                    pool.indirect_dma_start(owner_of, bass.IndirectOffsetOnAxis(ap=goal[:, c:c + 1], axis=0),
                                            edge_row[:, c:c + 1], None, bounds_check=NODES - 1,
                                            oob_is_err=False).then_inc(s["owners_put"], 16)
                pool.wait_ge(s["owners_put"], 16 * CHUNKS)
                for c in range(CHUNKS):
                    pool.indirect_dma_start(owner_i[:, c:c + 1], None, owner_of,
                                            bass.IndirectOffsetOnAxis(ap=src_col[:, c:c + 1], axis=0)
                                            ).then_inc(s["owners_got"], 16)
                pool.wait_ge(s["owners_got"], 16 * CHUNKS)

            @block.tensor
            def _(pe):
                pe.wait_ge(s["sources_in"], 16 * CHUNKS)
                for t in range(ETILES):
                    if t >= 2:
                        pe.wait_ge(s["first"], t - 1)
                    for j in range(PAIRS):
                        last = pe.transpose(bank[t % 2][:, j * P:(j + 1) * P],
                                            gathered_rows(t)[:, 2 * j * D:(2 * j + 2) * D], ident[0:P, 0:P])
                    last.then_inc(s["p"], 1)

            @block.scalar
            def _(act):
                for t in range(ETILES):
                    act.wait_ge(s["p"], t + 1)
                    act.activation(source_tile(t), bank[t % 2][:, 0:COLS], ACT.Copy).then_inc(s["first"], 1)
        finish_turn()
        with nc.Block() as block:
            kinds_block(block, type5, work, kind8, s)
        finish_turn()

        with nc.Fori(0, LAYERS) as turn:
            with nc.Block() as block:
                def load_weights_and_nodes(sp):
                    for half in range(2):
                        sp.dma_start(rel_now[64 * half:64 * half + 64, :, 64 * half:64 * half + 64],
                                     w_rel[turn].rearrange("r d k -> d r k")).then_inc(s["rel"], 16)
                    for k in range(GROUPS_A_TURN * GROUP):
                        sp.dma_start(tile_rows(k), x[bass.ds(turn * (GROUPS_A_TURN * GROUP * ROWS) + k * ROWS, ROWS), :]
                                     .rearrange("(p c) d -> p (c d)", c=CH)).then_inc(s["rows_in"], 16)
                message_engines(block, RELS, lambda r: rel_now[:, r, :],
                                lambda t: table[bass.ds(turn * EDGES + t * ROWS, ROWS), :]
                                .rearrange("(p c) d -> p (c d)", c=CH),
                                load_weights_and_nodes, indices_now)

            with nc.Block() as block:
                steps = []
                for grp in range(GROUPS_A_TURN):
                    tiles = range(grp * GROUP, (grp + 1) * GROUP)
                    steps += [Step(LOAD, k, x_buf[k % GROUP], rows=tile_rows(k)) for k in tiles]
                    for l in range(LAYERS):
                        steps += [Step(LAYER, k, x_buf[k % GROUP], w=w_all[:, l, :], vec=vec[:, l, :]) for k in tiles]
                    steps += [Step(SKIP, k, x_buf[k % GROUP], rows=tile_rows(k)) for k in tiles]
                    steps += [Step(LAST, k, x_buf[k % GROUP]) for k in tiles]
                    steps += [Step(OUT, k, x_buf[k % GROUP], rows=tile_rows(k)) for k in tiles]
                n_nodes = len(steps)
                steps += [Step(LAYER, 100 + t, source_tile(t), w=w_now[:, :], vec=vec_now[:, :],
                               agg=gathered_rows(t)) for t in range(ETILES)]
                number(steps)

                @block.sync
                def _(sp):
                    runs_on_sync(sp)
                    for st in steps:
                        if st.kind == OUT:
                            sp.wait_ge(s["first"], st.p + 1)
                            sp.dma_start(out[bass.ds(turn * (GROUPS_A_TURN * GROUP * ROWS) + st.tile * ROWS, ROWS), :]
                                         .rearrange("(p c) d -> p (c d)", c=CH), st.rows).then_inc(s["stored"], 16)
                    sp.wait_ge(s["stored"], 16 * GROUPS_A_TURN * GROUP)

                @block.gpsimd
                def _(pool):
                    runs_on_gather(pool)
                    runs_on_scatter(pool, turn)
                    for c in range(CHUNKS):
                        pool.indirect_dma_start(gathered[0:P, c * D:(c + 1) * D], None, sums_now,
                                                bass.IndirectOffsetOnAxis(ap=owner[:, c:c + 1], axis=0)
                                                ).then_inc(s["gathers"], 16)

                @block.tensor
                def _(pe):
                    pe.wait_ge(s["rows_in"], 16 * GROUPS_A_TURN * GROUP)

                    def agg_ready(pe, st):
                        if st is steps[n_nodes]:
                            pe.wait_ge(s["gathers"], turn * (16 * CHUNKS) + 16 * CHUNKS)
                            pe.wait_ge(s["now2"], 2)
                    stream_tensor(pe, steps, lambda: runs_on_tensor(pe), agg_ready)

                @block.scalar
                def _(act):
                    act.activation(w_now[:, :], w_all[:, turn, :], ACT.Copy).then_inc(s["now2"], 1)
                    act.wait_ge(s["now2"], 2)
                    stream_scalar(act, steps)

                @block.vector
                def _(dve):
                    dve.tensor_copy(vec_now[:, :], vec[:, turn, :]).then_inc(s["now2"], 1)
                    dve.wait_ge(s["now2"], 2)
                    stream_vector(dve, steps, lambda: runs_on_vector(dve, turn))
            finish_turn()

        with nc.Block() as block:
            steps = number([Step(ADD, t, source_tile(t), other=gathered[:, t * COLS:(t + 1) * COLS])
                            for t in range(ETILES)])
            w1_nat = rows[:, 0:RELS1 * 128].rearrange("p (r k) -> p r k", r=RELS1)

            @block.sync
            def _(sp):
                sp.dma_start(gathered[:, 0:ETILES * COLS], source_rows).then_inc(s["rows_in"], 16)
                sp.wait_ge(s["now"], 1)
                for half in range(2):
                    sp.dma_start(w1_nat[64 * half:64 * half + 64, :, 64 * half:64 * half + 64],
                                 w1.rearrange("r o f -> o r f")).then_inc(s["rel"], 16)
                sp.wait_ge(s["rel"], 32)

            @block.gpsimd
            def _(pool):
                pool.memset(rows[:, 0:RELS1 * 128], 0.0).then_inc(s["now"], 1)

            @block.tensor
            def _(pe):
                stream_tensor(pe, steps)

            @block.scalar
            def _(act):
                stream_scalar(act, steps)

            @block.vector
            def _(dve):
                dve.wait_ge(s["rows_in"], 16)
                stream_vector(dve, steps)
        finish_turn()

        w1_sb = gathered[:, 0:RELS1 * 128].rearrange("p (r k) -> p r k", r=RELS1)
        with nc.Block() as block:
            @block.tensor
            def _(pe):
                for r in range(RELS1):
                    last = pe.transpose(bank[r // 4][:, (r % 4) * 128:(r % 4 + 1) * 128], w1_nat[:, r, :], ident[:, :])
                last.then_inc(s["p"], 1)

            @block.scalar
            def _(act):
                act.wait_ge(s["p"], 1)
                for b in range(RELS1 // 4):
                    act.activation(gathered[:, b * 512:(b + 1) * 512], bank[b][:, :], ACT.Copy)
            kinds_block(block, type16, work, kind8, s)
        finish_turn()

        with nc.Block() as block:
            def rel_is_there(sp):
                sp.sem_inc(s["rel"], 32)
            message_engines(block, RELS1, lambda r: w1_sb[:, r, :],
                            lambda t: table[LAYERS * EDGES + t * ROWS:LAYERS * EDGES + (t + 1) * ROWS, :]
                            .rearrange("(p c) d -> p (c d)", c=CH),
                            rel_is_there, indices_now)
        with nc.Block() as block:
            @block.sync
            def _(sp):
                runs_on_sync(sp)

            @block.gpsimd
            def _(pool):
                runs_on_gather(pool)
                runs_on_scatter(pool, LAYERS)

            @block.tensor
            def _(pe):
                runs_on_tensor(pe)

            @block.vector
            def _(dve):
                runs_on_vector(dve, LAYERS)
        finish_turn()

        agg_buf = [gathered[0:P, i * CH * D:(i + 1) * CH * D] for i in range(6)]
        with nc.Fori(0, ETILES // GROUP) as turn:
            with nc.Block() as block:
                steps = [Step(LOAD, k, x_buf[k], rows=tile_rows(k)) for k in range(GROUP)]
                for l in range(LAYERS):
                    steps += [Step(LAYER, k, x_buf[k], w=w_all[:, l, :], vec=vec[:, l, :], layer=l) for k in range(GROUP)]
                steps += [Step(SKIP, k, x_buf[k], rows=tile_rows(k)) for k in range(GROUP)]
                steps += [Step(LAST, k, x_buf[k], rows=True, layer=LAYERS) for k in range(GROUP)]
                steps += [Step(OUT, k, x_buf[k], rows=tile_rows(k)) for k in range(GROUP)]
                number(steps)
                with_agg = [st for st in steps if st.kind in (LAYER, LAST)]
                for i, st in enumerate(with_agg):
                    st.order = i
                    if st.kind == LAYER:
                        st.agg = agg_buf[i % 6]
                    else:
                        st.rows = agg_buf[i % 6]

                @block.sync
                def _(sp):
                    for i, st in enumerate(with_agg):
                        if i >= 6:
                            sp.wait_ge(s["p"], with_agg[i - 6].p + 1)
                        sp.dma_start(agg_buf[i % 6], table[bass.ds(turn * (GROUP * ROWS) + (st.layer * EDGES + st.tile * ROWS), ROWS), :]
                                     .rearrange("(p c) d -> p (c d)", c=CH)).then_inc(s[f"agg{i % 6}"], 16)

                @block.gpsimd
                def _(pool):
                    pool.wait_ge(s["now2"], 2)
                    for c in range(GROUP * CH):
                        pool.indirect_dma_start(rows[0:P, c * D:(c + 1) * D], None, x,
                                                bass.IndirectOffsetOnAxis(ap=target_now[:, c:c + 1], axis=0)
                                                ).then_inc(s["targets_in"], 16)
                    for st in steps:
                        if st.kind == OUT:
                            pool.wait_ge(s["first"], st.p + 1)
                            for c in range(CH):
                                k = st.tile * CH + c
                                pool.indirect_dma_start(
                                    out, bass.IndirectOffsetOnAxis(ap=goal_now[:, k:k + 1], axis=0),
                                    rows[0:P, k * D:(k + 1) * D], None, bounds_check=NODES - 1,
                                    oob_is_err=False).then_inc(s["put"], 16)
                    pool.wait_ge(s["put"], turn * (16 * GROUP * CH) + 16 * GROUP * CH)

                @block.tensor
                def _(pe):
                    pe.wait_ge(s["targets_in"], turn * (16 * GROUP * CH) + 16 * GROUP * CH)

                    def agg_ready(pe, st):
                        if st.kind in (LAYER, LAST):
                            pe.wait_ge(s[f"agg{st.order % 6}"], 16 * (st.order // 6 + 1))
                    stream_tensor(pe, steps, agg_ready=agg_ready)

                @block.scalar
                def _(act):
                    stream_scalar(act, steps)

                @block.vector
                def _(dve):
                    dve.tensor_copy(target_now[:, :], target[:, bass.ds(turn * (GROUP * CH), GROUP * CH)]).then_inc(s["now2"], 1)
                    dve.tensor_copy(goal_now[:, :], goal[:, bass.ds(turn * (GROUP * CH), GROUP * CH)]).then_inc(s["now2"], 1)
                    stream_vector(dve, steps)
            finish_turn()


def kinds_block(block, edge_type, work, kind8, s):
    part = ETILES
    stage = work[:, 0:4 * COLS].bitcast(I32)
    by_chunk = edge_type.rearrange("(t j h p) -> h t j p", j=PAIRS, h=2, p=P)

    @block.sync
    def _(sp):
        for t in range(part):
            if t >= 4:
                sp.wait_ge(s["z"], t - 3)
            for h in range(2):
                sp.dma_start(stage[64 * h:64 * h + 64, (t % 4) * COLS:(t % 4 + 1) * COLS]
                             .rearrange("q (j p) -> q j p", j=PAIRS),
                             by_chunk[h, t].partition_broadcast(64)).then_inc(s[f"agg{t % 4}"], 16)

    @block.vector
    def _(dve):
        for t in range(part):
            dve.wait_ge(s[f"agg{t % 4}"], 32 * (t // 4 + 1))
            dve.tensor_copy(kind8[:, t * COLS:(t + 1) * COLS],
                            stage[:, (t % 4) * COLS:(t % 4 + 1) * COLS]).then_inc(s["z"], 1)


def kernel(**inputs):
    import concourse.bacc as _bacc
    from concourse.bass_utils import run_bass_kernel_spmd as _run

    names = ["x", "src", "dst", "edge_type_16", "edge_type_5", "L0_gnn_W_rel", "L0_gnn_W_root", "L0_gnn_bias",
             "L0_gnn_ln_gamma", "L0_gnn_ln_beta", "L1_gnn_W"]
    t, c = np.divmod(np.arange(CHUNKS), CH)
    places = np.zeros((Q, 4), np.float32)
    places[(c % 4) * ETILES + t, c // 4] = t * CH + c
    places[(c % 4) * ETILES + t, 2 + c // 4] = t * ROWS + c + ROWS
    nc = _bacc.Bacc("TRN2", target_bir_lowering=False, num_devices=1)
    arrays, args = {}, []
    for name in names:
        arrays["in_" + name] = np.ascontiguousarray(inputs[name])
    arrays["in_places"] = places
    for name, a in arrays.items():
        args.append(nc.dram_tensor(name, a.shape, mybir.dt.from_np(a.dtype), kind="ExternalInput").ap())
    args.append(nc.dram_tensor("out_0", (NODES, D), F32, kind="ExternalOutput").ap())
    build(nc, *args)
    r = _run(nc, [arrays], core_ids=[0])
    return r.results[0]["out_0"]
```

```python
from contextlib import ExitStack

import numpy as np

import concourse.bass as bass
from concourse import mybir

F32 = mybir.dt.float32
I32 = mybir.dt.int32
U32 = mybir.dt.uint32
U8 = mybir.dt.uint8
ALU = mybir.AluOpType
ACT = mybir.ActivationFunctionType

NODES, EDGES, D, LAYERS, RELS, RELS1 = 100000, 25000, 64, 10, 5, 16
EPS = 1e-5
P = 125
CH = 8
ROWS = P * CH
PAIRS = CH // 2
COLS = PAIRS * P
TILES = NODES // ROWS
ETILES = EDGES // ROWS
CHUNKS = EDGES // P
Q = CHUNKS // 2
GROUP = 5
EARLY = 4 * GROUP
NOW = (TILES - EARLY) // LAYERS
SLOTS = 2 * GROUP
TABLE = EDGES + 1
NOWHERE = float(1 << 20)

LOAD, LAYER, SKIP, LAST, ADD, OUT = "load", "layer", "skip", "last", "add", "out"


class Step:

    def __init__(self, kind, tile, x, w=None, vec=None, rows=None, agg=None, other=None, layer=0):
        self.kind, self.tile, self.x, self.w, self.vec = kind, tile, x, w, vec
        self.rows, self.agg, self.other, self.layer = rows, agg, other, layer
        self.p = self.n = self.a = self.before = self.before_out = None


def number(steps):
    p = n = a = 0
    last = {}
    for s in steps:
        s.before = last.get(s.tile)
        if s.kind != ADD and not (s.kind == LAST and s.rows is None):
            s.p = p
            p += 1
            last[s.tile] = ("first", p)
        if s.kind == ADD:
            s.a = a
            a += 1
        if s.kind not in (LOAD, OUT):
            s.n = n
            n += 1
            last[s.tile] = ("norm", n)
    return steps


def build(nc, x, src, dst, type16, type5, w_rel, w_root, bias, gamma, beta, w1, places, out):
    sums_now = nc.dram_tensor("message_sums_now", [TABLE, D], F32, kind="Internal").ap()
    table = nc.dram_tensor("message_sums_of_layers", [(LAYERS + 1) * EDGES, D], F32, kind="Internal").ap()
    owner_of = nc.dram_tensor("owner_of_node", [NODES, 1], I32, kind="Internal").ap()
    source_rows = nc.dram_tensor("source_rows", [128, ETILES * COLS], F32, kind="Internal").ap()

    with ExitStack() as ctx:
        def sb(name, shape, dt=F32):
            return ctx.enter_context(nc.sbuf_tensor(name, shape, dt))

        def sem(name):
            return ctx.enter_context(nc.semaphore(name))

        bank = [ctx.enter_context(nc.psum_tensor(f"bank{i}", [128, 512], F32)) for i in range(8)]
        source = sb("source", [128, ETILES * COLS])
        gathered = sb("gathered", [128, CHUNKS * D])
        same = sb("same", [P, CHUNKS * P], U8)
        kind8 = sb("kind8", [128, ETILES * COLS], U8)
        rows = sb("rows", [128, SLOTS * CH * D])
        work = sb("work", [128, 6600])
        w_all = sb("w_all", [128, LAYERS, 128])
        w_now = sb("w_now", [128, 128])
        rel_now = sb("rel_now", [128, RELS, 128])
        ident = sb("ident", [128, 128])
        center = sb("center", [128, 128])
        mean = sb("mean", [128, 128])
        vec = sb("vec", [128, LAYERS, 4])
        vec_now = sb("vec_now", [128, 4])
        eps = sb("eps", [128, 1])
        follows = sb("follows", [Q, 2, 2, Q])
        first_sum = sb("first_sum", [Q, 2, D])
        last_sum = sb("last_sum", [Q, 2, D])
        owner = sb("owner", [P, CHUNKS], U32)
        target = sb("target", [P, CHUNKS + GROUP * CH], U32)
        goal = sb("goal", [P, CHUNKS], U32)
        target_next = sb("target_next", [P, GROUP * CH], U32)
        goal_now = sb("goal_now", [P, GROUP * CH], U32)
        goal_before = sb("goal_before", [P, GROUP * CH], U32)
        last_owner = sb("last_owner", [Q, 2])
        last_owner_row = sb("last_owner_row", [Q, 2], U32)
        last_owner_now = sb("last_owner_now", [Q, 2], U32)
        base = sb("base", [128, 1])

        x_buf = [work[:, i * COLS:(i + 1) * COLS] for i in range(NOW)]
        sq_buf = [work[:, (NOW + i) * COLS:(NOW + 1 + i) * COLS] for i in range(2)]
        rstd_buf = [work[:, (NOW + 2 + i) * COLS:(NOW + 3 + i) * COLS] for i in range(2)]
        picked = [work[:, i * COLS:(i + 1) * COLS] for i in range(3)]
        sent = [work[:, (3 + i) * COLS:(4 + i) * COLS] for i in range(2)]
        sent_rows = [work[0:P, 2500 + i * 512:3012 + i * 512] for i in range(2)]
        same_f = [work[0:P, 3524 + i * 1000:4524 + i * 1000] for i in range(2)]
        sums = [work[0:P, 5524 + i * 512:6036 + i * 512] for i in range(2)]

        def tile_rows(k):
            return rows[0:P, k * CH * D:(k + 1) * CH * D]

        def gathered_rows(t):
            return gathered[0:P, t * CH * D:(t + 1) * CH * D]

        def source_tile(t):
            return source[:, t * COLS:(t + 1) * COLS]

        names = ("rows_in rows_in_odd p first add q square v ln rstd z norm stored corr_in corr corr_sum now now2 "
                 "rel picked sent sent_rows same_f sums mm turned summed store0 store1 agg0 agg1 agg2 agg3 agg4 "
                 "agg5 passed staged0 staged1 staged2 staged3 unstaged copied").split()
        s = {n: sem("s_" + n) for n in names}
        s.update({n: sem("s_" + n) for n in
                  "corr_got corr_put gathers put owners_put owners_got targets_in sources_in".split()})
        to_zero = range(s[names[0]].num, s[names[-1]].num + 1)

        def stream_tensor(pe, steps, hook=None, agg_ready=None):
            def turn(s_, rows_ap, dest):
                for j in range(PAIRS):
                    last = pe.transpose(dest[:, j * P:(j + 1) * P], rows_ap[:, 2 * j * D:(2 * j + 2) * D],
                                        ident[0:P, 0:P])
                return last

            for i in range(len(steps) + 2):
                if hook and i == 8:
                    hook()
                if i < len(steps) and steps[i].p is not None:
                    st = steps[i]
                    if st.p >= 2:
                        pe.wait_ge(s["first"], st.p - 1)
                    if st.before and st.kind in (LAYER, OUT):
                        pe.wait_ge(s[st.before[0]], st.before[1])
                    dest = bank[st.p % 2]
                    if agg_ready:
                        agg_ready(pe, st)
                    if st.kind in (LOAD, SKIP, LAST):
                        last = turn(st, st.rows, dest)
                    elif st.kind == OUT:
                        for j in range(PAIRS):
                            last = pe.transpose(dest[0:P, j * 128:(j + 1) * 128], st.x[:, j * P:(j + 1) * P],
                                                ident[:, :])
                    else:
                        last = pe.matmul(dest[:, 0:COLS], st.w, st.x, start=True, stop=st.agg is None,
                                         skip_group_check=True)
                        if st.agg is not None:
                            for j in range(PAIRS):
                                last = pe.matmul(dest[:, j * P:(j + 1) * P], st.agg[:, 2 * j * D:(2 * j + 2) * D],
                                                 ident[0:P, 0:P], start=False, stop=True, is_transpose=True,
                                                 skip_group_check=True)
                    last.then_inc(s["p"], 1)
                if 1 <= i <= len(steps) and steps[i - 1].n is not None:
                    st = steps[i - 1]
                    if st.n >= 3:
                        pe.wait_ge(s["norm"], st.n - 2)
                    if st.kind == ADD:
                        pe.wait_ge(s["add"], st.a + 1)
                    elif st.p is not None:
                        pe.wait_ge(s["first"], st.p + 1)
                    elif st.before:
                        pe.wait_ge(s[st.before[0]], st.before[1])
                    pe.matmul(bank[2 + st.n % 3][:, 0:COLS], center[:, :], st.x, start=True,
                              stop=True).then_inc(s["q"], 1)
                if i >= 2 and steps[i - 2].n is not None:
                    st = steps[i - 2]
                    pe.wait_ge(s["square"], st.n + 1)
                    if st.n >= 2:
                        pe.wait_ge(s["ln"], st.n - 1)
                    pe.matmul(bank[5 + st.n % 2][:, 0:COLS], mean[:, :], sq_buf[st.n % 2], start=True,
                              stop=True).then_inc(s["v"], 1)

        def stream_scalar(act, steps):
            act.preload_act_table_set("natural_log_exp_and_others")
            for i in range(len(steps) + 1):
                if i < len(steps) and steps[i].n is not None:
                    st = steps[i]
                    act.wait_ge(s["q"], st.n + 1)
                    if st.n >= 2:
                        act.wait_ge(s["v"], st.n - 1)
                    act.activation(sq_buf[st.n % 2], bank[2 + st.n % 3][:, 0:COLS], ACT.Square,
                                   bias=st.vec[:, 1:2] if st.kind == LAYER else 0.0).then_inc(s["square"], 1)
                if i >= 1 and steps[i - 1].n is not None:
                    k = steps[i - 1].n
                    act.wait_ge(s["v"], k + 1)
                    if k >= 2:
                        act.wait_ge(s["norm"], k - 1)
                    act.activation(rstd_buf[k % 2], bank[5 + k % 2][:, 0:COLS], ACT.Ln,
                                   bias=eps[:, 0:1]).then_inc(s["ln"], 1)
                    act.wait_ge(s["ln"], k + 1)
                    act.activation(rstd_buf[k % 2], rstd_buf[k % 2], ACT.Exp, scale=-0.5).then_inc(s["rstd"], 1)

        def stream_vector(dve, steps, hook=None, between=None):
            for i in range(len(steps) + 3):
                if hook and i == 10:
                    hook()
                if between:
                    between(i)
                if i < len(steps):
                    st = steps[i]
                    if st.p is not None:
                        dve.wait_ge(s["p"], st.p + 1)
                        pr = bank[st.p % 2]
                        if st.kind == LOAD:
                            done = dve.tensor_copy(st.x, pr[:, 0:COLS])
                        elif st.kind == OUT:
                            if st.before_out:
                                st.before_out(dve)
                            done = dve.tensor_copy(st.rows, pr[0:P, 0:CH * D])
                        elif st.kind == LAYER:
                            done = dve.scalar_tensor_tensor(out=st.x, in0=pr[:, 0:COLS], scalar=st.vec[:, 0:1],
                                                            in1=st.x, op0=ALU.max, op1=ALU.add)
                        else:
                            if st.before:
                                dve.wait_ge(s[st.before[0]], st.before[1])
                            done = dve.tensor_tensor(st.x, pr[:, 0:COLS], st.x, ALU.add)
                        done.then_inc(s["first"], 1)
                    elif st.kind == ADD:
                        dve.tensor_tensor(st.x, st.x, st.other, ALU.add).then_inc(s["add"], 1)
                if i >= 3 and steps[i - 3].n is not None:
                    st = steps[i - 3]
                    centered, rstd = bank[2 + st.n % 3][:, 0:COLS], rstd_buf[st.n % 2]
                    dve.wait_ge(s["rstd"], st.n + 1)
                    if st.kind == LAYER:
                        dve.scalar_tensor_tensor(out=st.x, in0=centered, scalar=st.vec[:, 1:2], in1=rstd,
                                                 op0=ALU.add, op1=ALU.mult).then_inc(s["z"], 1)
                        st_z = sum(1 for o in steps[:i - 2] if o.kind == LAYER)
                        dve.wait_ge(s["z"], st_z)
                        dve.tensor_scalar(st.x, st.x, st.vec[:, 2:3], st.vec[:, 3:4], ALU.mult,
                                          ALU.add).then_inc(s["norm"], 1)
                    else:
                        dve.tensor_tensor(st.x, centered, rstd, ALU.mult).then_inc(s["norm"], 1)

        def messages_sync(sp, table_rows):
            for t in range(ETILES):
                now = sums_now[t * ROWS:(t + 1) * ROWS, :].rearrange("(p c) d -> p (c d)", c=CH)
                sp.wait_ge(s["summed"], t + 1)
                sp.dma_start(table_rows(t), sums[t % 2]).then_inc(s[f"store{t % 2}"], 16)
                sp.dma_start(now, sums[t % 2]).then_inc(s[f"store{t % 2}"], 16)
            messages_stored(sp)

        def messages_stored(eng):
            eng.wait_ge(s["store0"], 32 * ((ETILES + 1) // 2))
            eng.wait_ge(s["store1"], 32 * (ETILES // 2))

        def messages_gpsimd(pool):
            for t in range(ETILES):
                if t >= 2:
                    pool.wait_ge(s["sums"], t - 1)
                pool.tensor_copy(same_f[t % 2], same[:, t * CH * P:(t + 1) * CH * P]).then_inc(s["same_f"], 1)

        def messages_vector(dve, rels):
            for t in range(ETILES):
                for r in range(rels):
                    k = t * rels + r
                    if k >= 3:
                        dve.wait_ge(s["mm"], k - 2)
                    dve.scalar_tensor_tensor(out=picked[k % 3], in0=kind8[:, t * COLS:(t + 1) * COLS],
                                             scalar=float(r), in1=source_tile(t), op0=ALU.is_equal,
                                             op1=ALU.mult).then_inc(s["picked"], 1)

        def messages_tensor(pe, rels, rel_tile):
            for i in range(ETILES + 2):
                if i < ETILES:
                    if i >= 2:
                        pe.wait_ge(s["sent"], i - 1)
                    for r in range(rels):
                        k = i * rels + r
                        pe.wait_ge(s["picked"], k + 1)
                        pe.matmul(bank[i % 2][:, 0:COLS], rel_tile(r), picked[k % 3], start=(r == 0),
                                  stop=(r == rels - 1)).then_inc(s["mm"], 1)
                if 1 <= i <= ETILES:
                    t = i - 1
                    pe.wait_ge(s["sent"], t + 1)
                    if t >= 2:
                        pe.wait_ge(s["sent_rows"], t - 1)
                    for j in range(PAIRS):
                        last = pe.transpose(bank[2 + t % 2][0:P, j * 128:(j + 1) * 128],
                                            sent[t % 2][:, j * P:(j + 1) * P], ident[:, :])
                    last.then_inc(s["turned"], 1)
                if i >= 2:
                    t = i - 2
                    pe.wait_ge(s["sent_rows"], t + 1)
                    pe.wait_ge(s["same_f"], t + 1)
                    if t >= 2:
                        pe.wait_ge(s["summed"], t - 1)
                    for c in range(CH):
                        last = pe.matmul(bank[4 + t % 2][0:P, c * D:(c + 1) * D],
                                         same_f[t % 2][:, c * P:(c + 1) * P],
                                         sent_rows[t % 2][:, c * D:(c + 1) * D], start=True, stop=True,
                                         skip_group_check=True)
                    last.then_inc(s["sums"], 1)

        def messages_read(pe):
            for n in ("sent", "sent_rows", "summed"):
                pe.wait_ge(s[n], ETILES)

        def messages_scalar(act, rels):
            for i in range(ETILES + 2):
                if i < ETILES:
                    act.wait_ge(s["mm"], rels * (i + 1))
                    if i >= 2:
                        act.wait_ge(s["turned"], i - 1)
                    act.activation(sent[i % 2], bank[i % 2][:, 0:COLS], ACT.Copy).then_inc(s["sent"], 1)
                if 1 <= i <= ETILES:
                    t = i - 1
                    act.wait_ge(s["turned"], t + 1)
                    if t >= 2:
                        act.wait_ge(s["sums"], t - 1)
                    act.activation(sent_rows[t % 2], bank[2 + t % 2][0:P, :], ACT.Copy).then_inc(s["sent_rows"], 1)
                if i >= 2:
                    t = i - 2
                    act.wait_ge(s["sums"], t + 1)
                    if t >= 2:
                        act.wait_ge(s[f"store{t % 2}"], 32 * (t // 2))
                    act.activation(sums[t % 2], bank[4 + t % 2][0:P, :], ACT.Copy).then_inc(s["summed"], 1)

        def kind_sync(sp, edge_type, t, stage, ring):
            by_half = edge_type.rearrange("(t j h p) -> h t j p", j=PAIRS, h=2, p=P)
            if t >= ring:
                sp.wait_ge(s["unstaged"], t - ring + 1)
            for h in range(2):
                sp.dma_start(stage[64 * h:64 * h + 64, (t % ring) * COLS:(t % ring + 1) * COLS]
                             .rearrange("q (j p) -> q j p", j=PAIRS),
                             by_half[h, t].partition_broadcast(64)).then_inc(s[f"staged{t % ring}"], 16)

        def kind_vector(dve, t, stage, ring):
            dve.wait_ge(s[f"staged{t % ring}"], 32 * (t // ring + 1))
            dve.tensor_copy(kind8[:, t * COLS:(t + 1) * COLS],
                            stage[:, (t % ring) * COLS:(t % ring + 1) * COLS]).then_inc(s["unstaged"], 1)

        def node_steps(tiles):
            tiles = list(tiles)
            buf = {k: x_buf[i] for i, k in enumerate(tiles)}
            steps = [Step(LOAD, k, buf[k], rows=tile_rows(k % SLOTS)) for k in tiles]
            for l in range(LAYERS):
                steps += [Step(LAYER, k, buf[k], w=w_all[:, l, :], vec=vec[:, l, :]) for k in tiles]
            steps += [Step(SKIP, k, buf[k], rows=tile_rows(k % SLOTS)) for k in tiles]
            steps += [Step(LAST, k, buf[k]) for k in tiles]
            return steps + [Step(OUT, k, buf[k], rows=tile_rows(k % SLOTS)) for k in tiles]

        def node_rows(a, first, k):
            at = first * ROWS + k * ROWS
            part = a[at:at + ROWS, :] if isinstance(at, int) else a[bass.ds(at, ROWS), :]
            return part.rearrange("(p c) d -> p (c d)", c=CH)

        def runs_on_sync(sp):
            for c in range(CH):
                q0 = (c % 4) * ETILES
                sp.dma_start(first_sum[q0:q0 + ETILES, c // 4, :],
                             sums_now[0:EDGES, :].rearrange("(t q) d -> t q d", q=ROWS)[:, c, :]
                             ).then_inc(s["corr_in"], 16)

        def runs_on_gather(pool):
            for h in range(2):
                pool.indirect_dma_start(last_sum[:, h, :], None, sums_now,
                                        bass.IndirectOffsetOnAxis(ap=last_owner_row[:, h:h + 1], axis=0)
                                        ).then_inc(s["corr_got"], 16)

        def runs_on_tensor(pe):
            pe.wait_ge(s["corr_in"], 16 * CH)
            for h in range(2):
                for k in range(2):
                    last = pe.matmul(bank[7][0:Q, h * D:(h + 1) * D], follows[:, k, h, :], first_sum[:, k, :],
                                     start=(h == 0 and k == 0), stop=(h == 1 and k == 1), skip_group_check=True)
            last.then_inc(s["corr"], 1)

        def runs_on_vector(dve, layer):
            dve.wait_ge(s["corr"], 1)
            dve.wait_ge(s["corr_got"], layer * 32 + 32)
            dve.tensor_tensor(last_sum[:, :, :].rearrange("q h d -> q (h d)"), bank[7][0:Q, 0:2 * D],
                              last_sum[:, :, :].rearrange("q h d -> q (h d)"), ALU.add).then_inc(s["corr_sum"], 1)

        def runs_on_scatter(pool, layer):
            pool.wait_ge(s["corr_sum"], 1)
            for to, at in ((sums_now, last_owner_row), (table, last_owner_now)):
                for h in range(2):
                    pool.indirect_dma_start(to, bass.IndirectOffsetOnAxis(ap=at[:, h:h + 1], axis=0),
                                            last_sum[:, h, :], None).then_inc(s["corr_put"], 16)
            pool.wait_ge(s["corr_put"], layer * 64 + 64)
            pool.sem_inc(s["passed"], 1)

        def indices_now(dve):
            dve.tensor_scalar(base[:, :], base[:, :], float(EDGES), None, ALU.add).then_inc(s["now"], 1)
            dve.wait_ge(s["now"], 1)
            dve.tensor_scalar(last_owner_now[:, :], last_owner[:, :], base[0:Q, :], None, ALU.add).then_inc(s["now"], 1)

        def finish_turn():
            nc.all_engine_barrier()
            nc.gpsimd.sem_clear(to_zero)
            nc.all_engine_barrier()

        def small(a, b, n=Q, dt=F32):
            v = work[0:n, a:b]
            return v if dt is F32 else v.bitcast(dt)

        half_chunks = 2 * P
        dst_i, prev_i, src_i = (small(k * half_chunks, (k + 1) * half_chunks, dt=I32) for k in range(3))
        dst_f, prev_f, src_f, own, goal_f, scratch = (small(k * half_chunks, (k + 1) * half_chunks) for k in range(3, 9))
        count = small(2250, 2252)
        last_diag, place_diag = small(2300, 2300 + 2 * Q), small(2500, 2500 + 2 * Q)
        ones = small(2700, 2700 + Q)
        after = small(4000, 4000 + 4 * Q)
        place = small(4400, 4404)
        no_owner = small(4500, 5300, P, I32)
        edge_row = small(3100, 3100 + CHUNKS, P, I32)
        dst_col = small(3300, 3300 + CHUNKS, P)
        zero_row = small(5400, 5400 + D, 1)
        bias_cols = small(5500, 5500 + LAYERS, 128)
        src_col = small(3500, 3500 + CHUNKS, P, U32)
        owner_i = small(3700, 3700 + CHUNKS, P, I32)

        def by_chunk(tile_, k):
            return tile_.rearrange("p (t c) -> p c t", c=CH)[:, 4 * k:4 * k + 4, :]

        with nc.Block() as block:
            @block.sync
            def _(sp):
                n = 0
                dst_t, src_t = (a.rearrange("(t q) -> t q", q=ROWS) for a in (dst, src))
                for c in range(CH):
                    q0, k0 = (c % 4) * ETILES, (c // 4) * P
                    sp.dma_start(dst_i[q0:q0 + ETILES, k0:k0 + P], dst_t[:, c * P:(c + 1) * P]).then_inc(s["rows_in"], 16)
                    sp.dma_start(src_i[q0:q0 + ETILES, k0:k0 + P], src_t[:, c * P:(c + 1) * P]).then_inc(s["rows_in"], 16)
                    if c:
                        sp.dma_start(prev_i[q0:q0 + ETILES, k0:k0 + P],
                                     dst_t[:, c * P - 1:(c + 1) * P - 1]).then_inc(s["rows_in"], 16)
                    n += 3 if c else 2
                sp.dma_start(prev_i[1:ETILES, 0:P], dst[ROWS - 1:EDGES - 1].rearrange("(t q) -> t q", q=ROWS)[:, 0:P]
                             ).then_inc(s["rows_in"], 16)
                sp.dma_start(prev_i[0:1, 1:P], dst[0:P - 1].rearrange("(a n) -> a n", a=1)).then_inc(s["rows_in"], 16)
                sp.dma_start(place, places).then_inc(s["rows_in"], 16)
                assert n + 3 == 26
                sp.wait_ge(s["same_f"], 5)
                for half in range(2):
                    part = slice(64 * half, 64 * half + 64)
                    sp.dma_start(w_all[part, :, part], w_root.rearrange("l d k -> d l k")).then_inc(s["rel"], 16)
                    for dest, a in ((bias_cols[part, :], bias), (vec[part, :, 2], gamma), (vec[part, :, 3], beta)):
                        sp.dma_start(dest, a.rearrange("l d -> d l"), allow_slow_non_contiguous=True).then_inc(s["rel"], 16)
                sp.dma_start(owner_of.rearrange("(p n) o -> p (n o)", p=P), no_owner).then_inc(s["stored"], 16)
                sp.dma_start(sums_now[EDGES:TABLE, :], zero_row).then_inc(s["stored"], 16)
                sp.wait_ge(s["stored"], 32)

            @block.gpsimd
            def _(pool):
                for a in (w_all[:, :, :], rel_now[:, :, :], center[:, :], mean[:, :], ident[:, :]):
                    last = pool.memset(a, 0.0)
                last.then_inc(s["picked"], 1)
                pool.wait_ge(s["picked"], 1)
                for half in range(2):
                    part = slice(64 * half, 64 * half + 64)
                    pool.memset(center[part, part], -1.0 / D)
                    pool.memset(mean[part, part], 1.0 / D).then_inc(s["picked"], 1)
                pool.wait_ge(s["picked"], 3)
                for a, v in ((ident[:, :], 1.0), (center[:, :], 1.0 - 1.0 / D)):
                    pool.affine_select(out=a, in_=a, compare_op=ALU.not_equal, fill=v, base=0,
                                       pattern=[[-1, 128]], channel_multiplier=1).then_inc(s["same_f"], 1)
                pool.memset(eps[:, :], EPS)
                pool.memset(base[:, :], -float(EDGES))
                pool.memset(ones, 1.0).then_inc(s["same_f"], 1)
                pool.memset(no_owner, EDGES).then_inc(s["same_f"], 1)
                pool.iota(edge_row, pattern=[[ROWS, ETILES], [1, CH]], base=0, channel_multiplier=CH)
                pool.memset(target[:, CHUNKS:], 0)
                pool.memset(goal_now[:, :], int(NOWHERE))
                pool.memset(zero_row, 0.0).then_inc(s["same_f"], 1)

            @block.vector
            def _(dve):
                done = [0]

                def then(ins):
                    done[0] += 1
                    ins.then_inc(s["z"], 1)
                    dve.wait_ge(s["z"], done[0])

                dve.wait_ge(s["rows_in"], 16 * 26)
                dve.memset(prev_i[0:1, 0:1], -1).then_inc(s["now"], 1)
                dve.wait_ge(s["now"], 1)
                dve.tensor_copy(dst_f, dst_i)
                dve.tensor_copy(src_f, src_i)
                then(dve.tensor_copy(prev_f, prev_i))
                then(dve.tensor_tensor(own, dst_f, prev_f, ALU.not_equal))
                then(dve.tensor_scalar(own, own, -NOWHERE, NOWHERE, ALU.mult, ALU.add))
                then(dve.tensor_tensor(goal_f, own, dst_f, ALU.add))
                for h in range(2):
                    then(dve.tensor_scalar(scratch[:, 0:P], dst_f[:, h * P:(h + 1) * P],
                                           dst_f[:, (h + 1) * P - 1:(h + 1) * P], None, ALU.is_equal, ALU.add,
                                           accum_out=count[:, h:h + 1]))
                then(dve.tensor_scalar(count, count, -float(CH), None, ALU.mult))
                dve.tensor_tensor(last_owner_row[:, :], count, place[:, 2:4], ALU.add)
                then(dve.tensor_tensor(last_owner[:, :], count, place[:, 2:4], ALU.add))
                dve.wait_ge(s["same_f"], 3)
                for h in range(2):
                    dve.tensor_scalar(last_diag[:, h * Q:(h + 1) * Q], ident[0:Q, 0:Q],
                                      dst_f[:, (h + 1) * P - 1:(h + 1) * P], None, ALU.mult)
                    then(dve.tensor_scalar(place_diag[:, h * Q:(h + 1) * Q], ident[0:Q, 0:Q], place[:, h:h + 1],
                                           None, ALU.mult))
                done_before_products = done[0]
                assert done_before_products == 10
                dve.wait_ge(s["p"], 1)
                for k in range(2):
                    psum = [bank[b][0:P, k * Q:(k + 1) * Q].rearrange("p (c t) -> p c t", c=4) for b in range(3)]
                    dve.tensor_copy(by_chunk(dst_col, k), psum[0])
                    dve.tensor_copy(by_chunk(target[:, 0:CHUNKS], k), psum[0])
                    dve.tensor_copy(by_chunk(goal[:, :], k), psum[1])
                    dve.tensor_copy(by_chunk(src_col, k), psum[2])
                for k in range(2):
                    for h in range(2):
                        a = after[:, (2 * k + h) * Q:(2 * k + h + 1) * Q]
                        then(dve.tensor_scalar(a, bank[4][0:Q, h * Q:(h + 1) * Q], place[:, k:k + 1], None, ALU.is_lt))
                        then(dve.scalar_tensor_tensor(out=follows[:, k, h, :], in0=bank[3][0:Q, h * Q:(h + 1) * Q],
                                                      scalar=dst_f[:, k * P:k * P + 1], in1=a, op0=ALU.is_equal,
                                                      op1=ALU.mult))
                dve.wait_ge(s["rel"], 16 * 8)
                dve.tensor_scalar(vec[:, :, 0], bias_cols, -1.0, None, ALU.mult)
                then(dve.tensor_copy(vec[:, :, 1], bank[5][:, 0:LAYERS]))

            @block.tensor
            def _(pe):
                pe.wait_ge(s["z"], 10)
                for k in range(2):
                    for b, a in enumerate((dst_f, goal_f, src_f)):
                        pe.transpose(bank[b][0:P, k * Q:(k + 1) * Q], a[:, k * P:(k + 1) * P], ident[0:Q, 0:Q])
                pe.matmul(bank[3][0:Q, 0:2 * Q], ones, last_diag, start=True, stop=True)
                pe.matmul(bank[4][0:Q, 0:2 * Q], ones, place_diag, start=True, stop=True)
                pe.wait_ge(s["rel"], 16 * 8)
                pe.matmul(bank[5][:, 0:LAYERS], center[:, :], bias_cols, start=True, stop=True).then_inc(s["p"], 1)
        finish_turn()

        with nc.Block() as block:
            dst_here = [source[0:P, i * ROWS:(i + 1) * ROWS].bitcast(I32) for i in range(2)]
            stage = source[:, 2 * ROWS:2 * ROWS + 2 * COLS].bitcast(I32)
            steps = []
            for g in range(0, EARLY, GROUP):
                steps += node_steps(range(g, g + GROUP))
            n_nodes = len(steps)
            steps += [Step(LOAD, TILES + t, source_tile(t), rows=gathered_rows(t)) for t in range(ETILES)]
            number(steps)
            apart = n_nodes // (2 * ETILES + 2)
            loaded = ["rows_in", "rows_in_odd"]

            @block.sync
            def _(sp):
                def load(k):
                    sp.dma_start(tile_rows(k % SLOTS), node_rows(x, 0, k)).then_inc(s[loaded[k // GROUP % 2]], 16)

                for k in range(SLOTS):
                    load(k)
                for i, st in enumerate(steps):
                    if i % apart == 0 and i // apart < 2 * ETILES:
                        t = i // apart // 2
                        if i // apart % 2:
                            kind_sync(sp, type5, t, stage, 2)
                        else:
                            if t >= 2:
                                sp.wait_ge(s["same_f"], t - 1)
                            sp.dma_start(dst_here[t % 2], dst[t * ROWS:(t + 1) * ROWS].partition_broadcast(P)
                                         ).then_inc(s[f"agg{t % 2}"], 16)
                    if st.kind == OUT:
                        sp.wait_ge(s["first"], st.p + 1)
                        sp.dma_start(node_rows(out, 0, st.tile), st.rows).then_inc(s["stored"], 16)
                        if (st.tile + 1) % GROUP == 0 and st.tile + GROUP < EARLY - 1:
                            sp.wait_ge(s["stored"], 16 * (st.tile + 1))
                            for k in range(st.tile + 1 + GROUP, st.tile + 1 + 2 * GROUP):
                                load(k)
                sp.wait_ge(s["first"], steps[-1].p + 1)
                sp.dma_start(source_rows, source[:, :]).then_inc(s["stored"], 16)
                sp.wait_ge(s["stored"], 16 * EARLY + 16)

            @block.gpsimd
            def _(pool):
                for c in range(CHUNKS):
                    pool.indirect_dma_start(gathered[0:P, c * D:(c + 1) * D], None, x,
                                            bass.IndirectOffsetOnAxis(ap=src_col[:, c:c + 1], axis=0)
                                            ).then_inc(s["sources_in"], 16)
                for c in range(CHUNKS):
                    pool.indirect_dma_start(owner_of, bass.IndirectOffsetOnAxis(ap=goal[:, c:c + 1], axis=0),
                                            edge_row[:, c:c + 1], None, bounds_check=NODES - 1,
                                            oob_is_err=False).then_inc(s["owners_put"], 16)
                pool.wait_ge(s["owners_put"], 16 * CHUNKS)
                for c in range(CHUNKS):
                    pool.indirect_dma_start(owner_i[:, c:c + 1], None, owner_of,
                                            bass.IndirectOffsetOnAxis(ap=src_col[:, c:c + 1], axis=0)
                                            ).then_inc(s["owners_got"], 16)
                pool.wait_ge(s["owners_got"], 16 * CHUNKS)

            @block.tensor
            def _(pe):
                def ready(pe, st):
                    if st.kind == LOAD and st.tile < TILES and st.tile % GROUP == 0:
                        g = st.tile // GROUP
                        pe.wait_ge(s[loaded[g % 2]], 16 * GROUP * (g // 2 + 1))
                    if st is steps[n_nodes]:
                        pe.wait_ge(s["sources_in"], 16 * CHUNKS)
                stream_tensor(pe, steps, agg_ready=ready)

            @block.scalar
            def _(act):
                stream_scalar(act, steps)

            @block.vector
            def _(dve):
                def indices(i):
                    f = i // apart - 1
                    if i % apart or not 0 <= f < 2 * ETILES:
                        return
                    t = f // 2
                    if f % 2:
                        kind_vector(dve, t, stage, 2)
                        return
                    dve.wait_ge(s[f"agg{t % 2}"], 16 * (t // 2 + 1))
                    for c in range(CH):
                        k = t * CH + c
                        last = dve.tensor_scalar(same[:, k * P:(k + 1) * P], dst_here[t % 2][:, c * P:(c + 1) * P],
                                                 dst_col[:, k:k + 1], None, ALU.is_equal)
                    last.then_inc(s["same_f"], 1)

                stream_vector(dve, steps, between=indices)
                dve.wait_ge(s["owners_got"], 16 * CHUNKS)
                dve.tensor_copy(owner[:, :], owner_i)
        finish_turn()

        with nc.Fori(0, LAYERS) as turn:
            with nc.Block() as block:
                steps = node_steps(range(NOW))
                n_nodes = len(steps)
                steps += [Step(LAYER, TILES + t, source_tile(t), w=w_now[:, :], vec=vec_now[:, :],
                               agg=gathered_rows(t)) for t in range(ETILES)]
                number(steps)
                first_tile = turn * NOW + EARLY

                @block.sync
                def _(sp):
                    for half in range(2):
                        sp.dma_start(rel_now[64 * half:64 * half + 64, :, 64 * half:64 * half + 64],
                                     w_rel[turn].rearrange("r d k -> d r k")).then_inc(s["rel"], 16)
                    for k in range(NOW):
                        sp.dma_start(tile_rows(k), node_rows(x, first_tile, k)).then_inc(s["rows_in"], 16)
                    messages_sync(sp, lambda t: table[bass.ds(turn * EDGES + t * ROWS, ROWS), :]
                                  .rearrange("(p c) d -> p (c d)", c=CH))
                    runs_on_sync(sp)
                    for st in steps:
                        if st.kind == OUT:
                            sp.wait_ge(s["first"], st.p + 1)
                            sp.dma_start(node_rows(out, first_tile, st.tile), st.rows).then_inc(s["stored"], 16)
                    sp.wait_ge(s["stored"], 16 * NOW)

                @block.gpsimd
                def _(pool):
                    messages_gpsimd(pool)
                    messages_stored(pool)
                    pool.wait_ge(s["now"], 2)
                    runs_on_gather(pool)
                    runs_on_scatter(pool, turn)
                    for c in range(CHUNKS):
                        pool.indirect_dma_start(gathered[0:P, c * D:(c + 1) * D], None, sums_now,
                                                bass.IndirectOffsetOnAxis(ap=owner[:, c:c + 1], axis=0)
                                                ).then_inc(s["gathers"], 16)

                @block.tensor
                def _(pe):
                    pe.wait_ge(s["rel"], 32)
                    messages_tensor(pe, RELS, lambda r: rel_now[:, r, :])
                    messages_read(pe)
                    pe.wait_ge(s["rows_in"], 16 * NOW)

                    def ready(pe, st):
                        if st is steps[n_nodes]:
                            pe.wait_ge(s["gathers"], turn * (16 * CHUNKS) + 16 * CHUNKS)
                            pe.wait_ge(s["now2"], 2)
                    stream_tensor(pe, steps, lambda: runs_on_tensor(pe), ready)

                @block.scalar
                def _(act):
                    messages_scalar(act, RELS)
                    act.activation(w_now[:, :], w_all[:, turn, :], ACT.Copy).then_inc(s["now2"], 1)
                    messages_stored(act)
                    act.wait_ge(s["now2"], 2)
                    stream_scalar(act, steps)

                @block.vector
                def _(dve):
                    indices_now(dve)
                    messages_vector(dve, RELS)
                    dve.tensor_copy(vec_now[:, :], vec[:, turn, :]).then_inc(s["now2"], 1)
                    dve.wait_ge(s["now2"], 2)
                    stream_vector(dve, steps, lambda: runs_on_vector(dve, turn))
            finish_turn()

        w1_nat, w1_sb = (rows[:, i * RELS1 * 128:(i + 1) * RELS1 * 128].rearrange("p (r k) -> p r k", r=RELS1)
                         for i in range(2))
        with nc.Block() as block:
            steps = number([Step(ADD, t, source_tile(t), other=gathered[:, t * COLS:(t + 1) * COLS])
                            for t in range(ETILES)])
            stage = work[:, 0:4 * COLS].bitcast(I32)

            @block.sync
            def _(sp):
                sp.dma_start(gathered[:, 0:ETILES * COLS], source_rows).then_inc(s["rows_in"], 16)
                sp.wait_ge(s["now"], 1)
                for half in range(2):
                    sp.dma_start(w1_nat[64 * half:64 * half + 64, :, 64 * half:64 * half + 64],
                                 w1.rearrange("r o f -> o r f")).then_inc(s["rel"], 16)
                for t in range(ETILES):
                    kind_sync(sp, type16, t, stage, 4)

            @block.gpsimd
            def _(pool):
                pool.memset(rows[:, 0:RELS1 * 128], 0.0).then_inc(s["now"], 1)

            @block.tensor
            def _(pe):
                stream_tensor(pe, steps)
                pe.wait_ge(s["rel"], 32)
                pe.wait_ge(s["norm"], ETILES)
                for r in range(RELS1):
                    last = pe.transpose(bank[r // 4][:, (r % 4) * 128:(r % 4 + 1) * 128], w1_nat[:, r, :], ident[:, :])
                last.then_inc(s["turned"], 1)

            @block.scalar
            def _(act):
                stream_scalar(act, steps)
                act.wait_ge(s["turned"], 1)
                for b in range(RELS1 // 4):
                    act.activation(w1_sb[:, 4 * b:4 * b + 4, :].rearrange("p r k -> p (r k)"), bank[b][:, :], ACT.Copy)

            @block.vector
            def _(dve):
                dve.wait_ge(s["rows_in"], 16)
                stream_vector(dve, steps, between=lambda i: kind_vector(dve, i, stage, 4) if i < ETILES else None)
        finish_turn()

        next_rows = gathered[0:P, GROUP * CH * D * 2:GROUP * CH * D * 3]

        def gather_targets(pool, index):
            for c in range(GROUP * CH):
                pool.indirect_dma_start(next_rows[:, c * D:(c + 1) * D], None, x,
                                        bass.IndirectOffsetOnAxis(ap=index[:, c:c + 1], axis=0)
                                        ).then_inc(s["targets_in"], 16)

        def scatter_targets(pool, index):
            for c in range(GROUP * CH):
                at = GROUP * CH + c
                pool.indirect_dma_start(out, bass.IndirectOffsetOnAxis(ap=index[:, c:c + 1], axis=0),
                                        rows[0:P, at * D:(at + 1) * D], None, bounds_check=NODES - 1,
                                        oob_is_err=False).then_inc(s["put"], 16)

        with nc.Block() as block:
            @block.sync
            def _(sp):
                messages_sync(sp, lambda t: table[LAYERS * EDGES + t * ROWS:LAYERS * EDGES + (t + 1) * ROWS, :]
                              .rearrange("(p c) d -> p (c d)", c=CH))
                runs_on_sync(sp)

            @block.gpsimd
            def _(pool):
                messages_gpsimd(pool)
                messages_stored(pool)
                pool.wait_ge(s["now"], 2)
                runs_on_gather(pool)
                gather_targets(pool, target)
                runs_on_scatter(pool, LAYERS)

            @block.tensor
            def _(pe):
                messages_tensor(pe, RELS1, lambda r: w1_sb[:, r, :])
                runs_on_tensor(pe)

            @block.scalar
            def _(act):
                messages_scalar(act, RELS1)

            @block.vector
            def _(dve):
                indices_now(dve)
                messages_vector(dve, RELS1)
                runs_on_vector(dve, LAYERS)
        finish_turn()

        ring = 5
        agg_buf = [gathered[0:P, i * CH * D:(i + 1) * CH * D] for i in range(ring)]
        with nc.Fori(0, ETILES // GROUP) as turn:
            with nc.Block() as block:
                steps = [Step(LOAD, k, x_buf[k], rows=tile_rows(k)) for k in range(GROUP)]
                for l in range(LAYERS):
                    steps += [Step(LAYER, k, x_buf[k], w=w_all[:, l, :], vec=vec[:, l, :], layer=l) for k in range(GROUP)]
                steps += [Step(SKIP, k, x_buf[k], rows=tile_rows(k)) for k in range(GROUP)]
                steps += [Step(LAST, k, x_buf[k], rows=True, layer=LAYERS) for k in range(GROUP)]
                steps += [Step(OUT, k, x_buf[k], rows=tile_rows(GROUP + k)) for k in range(GROUP)]
                number(steps)
                with_agg = [st for st in steps if st.kind in (LAYER, LAST)]
                for i, st in enumerate(with_agg):
                    st.order = i
                    if st.kind == LAYER:
                        st.agg = agg_buf[i % ring]
                    else:
                        st.rows = agg_buf[i % ring]
                for st in steps:
                    if st.kind == OUT and st.tile == 0:
                        st.before_out = lambda dve: dve.wait_ge(s["put"], turn * (16 * GROUP * CH) + 16 * GROUP * CH)

                @block.sync
                def _(sp):
                    for i, st in enumerate(with_agg):
                        if i >= ring:
                            sp.wait_ge(s["p"], with_agg[i - ring].p + 1)
                        sp.dma_start(agg_buf[i % ring], table[bass.ds(turn * (GROUP * ROWS) + (st.layer * EDGES + st.tile * ROWS), ROWS), :]
                                     .rearrange("(p c) d -> p (c d)", c=CH)).then_inc(s[f"agg{i % ring}"], 16)

                @block.gpsimd
                def _(pool):
                    pool.wait_ge(s["now2"], 2)
                    scatter_targets(pool, goal_before)
                    pool.wait_ge(s["copied"], GROUP)
                    gather_targets(pool, target_next)

                @block.tensor
                def _(pe):
                    def ready(pe, st):
                        if st.kind == LOAD:
                            pe.wait_ge(s["copied"], st.tile + 1)
                        if st.kind in (LAYER, LAST):
                            pe.wait_ge(s[f"agg{st.order % ring}"], 16 * (st.order // ring + 1))
                    stream_tensor(pe, steps, agg_ready=ready)

                @block.scalar
                def _(act):
                    act.wait_ge(s["targets_in"], turn * (16 * GROUP * CH) + 16 * GROUP * CH)
                    for k in range(GROUP):
                        act.activation(tile_rows(k), next_rows[:, k * CH * D:(k + 1) * CH * D], ACT.Copy).then_inc(s["copied"], 1)
                    stream_scalar(act, steps)

                @block.vector
                def _(dve):
                    n = GROUP * CH
                    dve.tensor_copy(goal_before[:, :], goal_now[:, :]).then_inc(s["now2"], 1)
                    dve.tensor_copy(target_next[:, :], target[:, bass.ds(turn * n + n, n)]).then_inc(s["now2"], 1)
                    dve.wait_ge(s["now2"], 2)
                    dve.tensor_copy(goal_now[:, :], goal[:, bass.ds(turn * n, n)]).then_inc(s["now2"], 1)
                    stream_vector(dve, steps)
            finish_turn()

        with nc.Block() as block:
            @block.gpsimd
            def _(pool):
                scatter_targets(pool, goal_now)
                pool.wait_ge(s["put"], 16 * GROUP * CH * (ETILES // GROUP + 1))
                pool.wait_ge(s["targets_in"], 16 * GROUP * CH * (ETILES // GROUP + 1))


def kernel(**inputs):
    import concourse.bacc as _bacc
    from concourse.bass_utils import run_bass_kernel_spmd as _run

    names = ["x", "src", "dst", "edge_type_16", "edge_type_5", "L0_gnn_W_rel", "L0_gnn_W_root", "L0_gnn_bias",
             "L0_gnn_ln_gamma", "L0_gnn_ln_beta", "L1_gnn_W"]
    t, c = np.divmod(np.arange(CHUNKS), CH)
    places = np.zeros((Q, 4), np.float32)
    places[(c % 4) * ETILES + t, c // 4] = t * CH + c
    places[(c % 4) * ETILES + t, 2 + c // 4] = t * ROWS + c + ROWS
    nc = _bacc.Bacc("TRN2", target_bir_lowering=False, num_devices=1)
    arrays, args = {}, []
    for name in names:
        arrays["in_" + name] = np.ascontiguousarray(inputs[name])
    arrays["in_places"] = places
    for name, a in arrays.items():
        args.append(nc.dram_tensor(name, a.shape, mybir.dt.from_np(a.dtype), kind="ExternalInput").ap())
    args.append(nc.dram_tensor("out_0", (NODES, D), F32, kind="ExternalOutput").ap())
    build(nc, *args)
    r = _run(nc, [arrays], core_ids=[0])
    return r.results[0]["out_0"]
```

```python
from contextlib import ExitStack

import numpy as np

import concourse.bass as bass
from concourse import mybir

F32 = mybir.dt.float32
F32R = mybir.dt.float32r
I32 = mybir.dt.int32
U32 = mybir.dt.uint32
U8 = mybir.dt.uint8
ALU = mybir.AluOpType
ACT = mybir.ActivationFunctionType

NODES, EDGES, D, LAYERS, RELS, RELS1 = 100000, 25000, 64, 10, 5, 16
EPS = 1e-5
P = 125
CH = 8
ROWS = P * CH
PAIRS = CH // 2
COLS = PAIRS * P
TILES = NODES // ROWS
ETILES = EDGES // ROWS
CHUNKS = EDGES // P
Q = CHUNKS // 2
EARLY_GROUPS = (7, 7, 6)
EARLY = sum(EARLY_GROUPS)
NOW = (TILES - EARLY) // LAYERS
PORTION = 5
TARGET_GROUPS = (9, 9, 7)
SLOTS = 10
TABLE = EDGES + 1
WHOLE = 6
NOWHERE = float(1 << 20)

LOAD, LAYER, SKIP, LAST, ADD, OUT = "load", "layer", "skip", "last", "add", "out"


class Step:

    def __init__(self, kind, tile, x, w=None, vec=None, rows=None, agg=None, other=None, layer=0):
        self.kind, self.tile, self.x, self.w, self.vec = kind, tile, x, w, vec
        self.rows, self.agg, self.other, self.layer = rows, agg, other, layer
        self.p = self.n = self.l = self.h = self.a = self.before = None


def number(steps):
    p = n = l = h = a = plain = 0
    last = {}
    for s in steps:
        s.before = last.get(s.tile)
        if s.kind != ADD and not (s.kind == LAST and s.rows is None):
            s.p = p
            p += 1
            last[s.tile] = ("first", p)
        if s.kind == ADD:
            s.a = a
            a += 1
        if s.kind not in (LOAD, OUT):
            plain += s.agg is None
            if s.kind == LAYER and (s.agg is not None or plain % WHOLE):
                s.h = h
                h += 1
            s.n = n
            n += 1
            last[s.tile] = ("z", n)
        if s.kind == LAYER:
            s.l = l
            l += 1
            last[s.tile] = ("norm", l)
    return steps


def build(nc, x, src, dst, type16, type5, w_rel, w_root, bias, gamma, beta, w1, places, out):
    sums_now = nc.dram_tensor("message_sums_now", [TABLE, D], F32, kind="Internal").ap()
    table = nc.dram_tensor("message_sums_of_layers", [(LAYERS + 1) * EDGES, D], F32, kind="Internal").ap()
    owner_of = nc.dram_tensor("owner_of_node", [NODES, 1], I32, kind="Internal").ap()
    source_rows = nc.dram_tensor("source_rows", [128, ETILES * COLS], F32, kind="Internal").ap()

    with ExitStack() as ctx:
        def sb(name, shape, dt=F32):
            return ctx.enter_context(nc.sbuf_tensor(name, shape, dt))

        def sem(name):
            return ctx.enter_context(nc.semaphore(name))

        bank = [ctx.enter_context(nc.psum_tensor(f"bank{i}", [128, 512], F32)) for i in range(8)]
        source = sb("source", [128, ETILES * COLS])
        gathered = sb("gathered", [128, CHUNKS * D])
        same = sb("same", [P, CHUNKS * P], U8)
        kind8 = sb("kind8", [128, ETILES * COLS], U8)
        rows = sb("rows", [128, SLOTS * CH * D])
        work = sb("work", [128, 6800])
        w_all = sb("w_all", [128, LAYERS, 128])
        w_now = sb("w_now", [128, 128])
        rel_now = sb("rel_now", [128, RELS, 128])
        ident = sb("ident", [128, 128])
        center = sb("center", [128, 128])
        center_r = sb("center_r", [128, 128], F32R)
        high = [sb(f"high{i}", [128, COLS], F32R) for i in range(2)]
        low = [sb(f"low{i}", [128, COLS], F32R) for i in range(2)]
        mean = sb("mean", [128, 128])
        vec = sb("vec", [128, LAYERS, 4])
        vec_now = sb("vec_now", [128, 4])
        eps = sb("eps", [128, 1])
        follows = sb("follows", [Q, 2, 2, Q])
        first_sum = sb("first_sum", [Q, 2, D])
        last_sum = sb("last_sum", [Q, 2, D])
        owner = sb("owner", [P, CHUNKS], U32)
        target = sb("target", [P, CHUNKS], U32)
        goal = sb("goal", [P, CHUNKS], U32)
        last_owner = sb("last_owner", [Q, 2])
        last_owner_row = sb("last_owner_row", [Q, 2], U32)
        last_owner_now = sb("last_owner_now", [Q, 2], U32)
        base = sb("base", [128, 1])

        x_buf = [work[:, i * COLS:(i + 1) * COLS] for i in range(NOW)]
        sq_buf = [work[:, (NOW + i) * COLS:(NOW + 1 + i) * COLS] for i in range(2)]
        rstd_buf = [work[:, (NOW + 2 + i) * COLS:(NOW + 3 + i) * COLS] for i in range(2)]
        picked = [work[:, i * COLS:(i + 1) * COLS] for i in range(3)]
        sent = [work[:, (3 + i) * COLS:(4 + i) * COLS] for i in range(2)]
        sent_rows = [work[0:P, 2500 + i * 512:3012 + i * 512] for i in range(2)]
        same_f = [work[0:P, 3524 + i * 1000:4524 + i * 1000] for i in range(2)]
        sums = [work[0:P, 5524 + i * 512:6036 + i * 512] for i in range(2)]

        def tile_rows(k):
            return rows[0:P, k * CH * D:(k + 1) * CH * D]

        def gathered_rows(t):
            return gathered[0:P, t * CH * D:(t + 1) * CH * D]

        def source_tile(t):
            return source[:, t * COLS:(t + 1) * COLS]

        names = ("rows_in slot0 slot1 slot2 slot3 slot4 slot5 slot6 slot7 slot8 slot9 stored "
                 "p first add high low q square v ln rstd z norm corr_in corr corr_sum now now2 "
                 "rel picked sent sent_rows same_f sums mm turned summed store0 store1 agg0 agg1 agg2 agg3 agg4 "
                 "passed staged0 staged1 staged2 staged3 unstaged").split()
        s = {n: sem("s_" + n) for n in names}
        s.update({n: sem("s_" + n) for n in
                  ("corr_got corr_put gathers0 gathers1 gathers2 gathers3 gathers4 put owners_put "
                   "owners_got targets_in sources_in").split()})
        to_zero = range(s[names[0]].num, s[names[-1]].num + 1)

        def stream_tensor(pe, steps, hook=None, agg_ready=None):
            def turn(s_, rows_ap, dest):
                for j in range(PAIRS):
                    last = pe.transpose(dest[:, j * P:(j + 1) * P], rows_ap[:, 2 * j * D:(2 * j + 2) * D],
                                        ident[0:P, 0:P])
                return last

            for i in range(len(steps) + 4):
                if hook and i == 10:
                    hook()
                if i < len(steps) and steps[i].p is not None:
                    st = steps[i]
                    if st.p >= 2:
                        pe.wait_ge(s["first"], st.p - 1)
                    if st.before and st.kind in (LAYER, OUT):
                        pe.wait_ge(s[st.before[0]], st.before[1])
                    dest = bank[st.p % 2]
                    if agg_ready:
                        agg_ready(pe, st)
                    if st.kind in (LOAD, SKIP, LAST):
                        last = turn(st, st.rows, dest)
                    elif st.kind == OUT:
                        for j in range(PAIRS):
                            last = pe.transpose(dest[0:P, j * 128:(j + 1) * 128], st.x[:, j * P:(j + 1) * P],
                                                ident[:, :])
                    else:
                        last = pe.matmul(dest[:, 0:COLS], st.w, st.x, start=True, stop=st.agg is None,
                                         skip_group_check=True)
                        if st.agg is not None:
                            for j in range(PAIRS):
                                last = pe.matmul(dest[:, j * P:(j + 1) * P], st.agg[:, 2 * j * D:(2 * j + 2) * D],
                                                 ident[0:P, 0:P], start=False, stop=True, is_transpose=True,
                                                 skip_group_check=True)
                    last.then_inc(s["p"], 1)
                if 3 <= i < len(steps) + 3 and steps[i - 3].n is not None:
                    st = steps[i - 3]
                    dest = bank[2 + st.n % 3][:, 0:COLS]
                    if st.n >= 3:
                        pe.wait_ge(s["z"], st.n - 2)
                    if st.h is None:
                        summed(pe, st)
                        pe.matmul(dest, center[:, :], st.x, start=True, stop=True).then_inc(s["q"], 1)
                    else:
                        pe.wait_ge(s["low"], st.h + 1)
                        pe.matmul(dest, center_r[:, :], high[st.h % 2][:, :], start=True, stop=False)
                        pe.matmul(dest, center_r[:, :], low[st.h % 2][:, :], start=False,
                                  stop=True).then_inc(s["q"], 1)
                if i >= 4 and steps[i - 4].n is not None:
                    st = steps[i - 4]
                    pe.wait_ge(s["square"], st.n + 1)
                    if st.n >= 2:
                        pe.wait_ge(s["ln"], st.n - 1)
                    pe.matmul(bank[5 + st.n % 2][:, 0:COLS], mean[:, :], sq_buf[st.n % 2], start=True,
                              stop=True).then_inc(s["v"], 1)

        def summed(eng, st):
            if st.kind == ADD:
                eng.wait_ge(s["add"], st.a + 1)
            elif st.p is not None:
                eng.wait_ge(s["first"], st.p + 1)
            elif st.before:
                eng.wait_ge(s[st.before[0]], st.before[1])

        def half_used(eng, steps, st):
            for o in steps:
                if o.h is not None and o.h == st.h - 2:
                    eng.wait_ge(s["q"], o.n + 1)

        def stream_scalar(act, steps):
            for i in range(len(steps) + 4):
                if 3 <= i < len(steps) + 3 and steps[i - 3].n is not None:
                    st = steps[i - 3]
                    act.wait_ge(s["q"], st.n + 1)
                    if st.n >= 2:
                        act.wait_ge(s["v"], st.n - 1)
                    act.activation(sq_buf[st.n % 2], bank[2 + st.n % 3][:, 0:COLS], ACT.Square,
                                   bias=st.vec[:, 1:2] if st.kind == LAYER else 0.0).then_inc(s["square"], 1)
                if 1 <= i <= len(steps) and steps[i - 1].h is not None:
                    st = steps[i - 1]
                    summed(act, st)
                    half_used(act, steps, st)
                    act.activation(high[st.h % 2][:, :], st.x, ACT.Copy).then_inc(s["high"], 1)
                if i >= 4 and steps[i - 4].n is not None:
                    k = steps[i - 4].n
                    act.wait_ge(s["v"], k + 1)
                    if k >= 2:
                        act.wait_ge(s["z"], k - 1)
                    act.activation(rstd_buf[k % 2], bank[5 + k % 2][:, 0:COLS], ACT.Ln,
                                   bias=eps[:, 0:1]).then_inc(s["ln"], 1)
                    act.wait_ge(s["ln"], k + 1)
                    act.activation(rstd_buf[k % 2], rstd_buf[k % 2], ACT.Exp, scale=-0.5).then_inc(s["rstd"], 1)

        def stream_vector(dve, steps, hook=None, between=None):
            for i in range(len(steps) + 6):
                if hook and i == 12:
                    hook()
                if between:
                    between(i)
                if i >= 6 and steps[i - 6].l is not None:
                    st = steps[i - 6]
                    dve.wait_ge(s["z"], st.n + 1)
                    dve.tensor_scalar(st.x, st.x, st.vec[:, 2:3], st.vec[:, 3:4], ALU.mult,
                                      ALU.add).then_inc(s["norm"], 1)
                if 2 <= i < len(steps) + 2 and steps[i - 2].h is not None:
                    st = steps[i - 2]
                    dve.wait_ge(s["high"], st.h + 1)
                    half_used(dve, steps, st)
                    dve.tensor_tensor(low[st.h % 2][:, :], st.x, high[st.h % 2][:, :].bitcast(F32),
                                      ALU.subtract).then_inc(s["low"], 1)
                if 5 <= i < len(steps) + 5 and steps[i - 5].n is not None:
                    st = steps[i - 5]
                    centered, rstd = bank[2 + st.n % 3][:, 0:COLS], rstd_buf[st.n % 2]
                    dve.wait_ge(s["rstd"], st.n + 1)
                    if st.kind == LAYER:
                        done = dve.scalar_tensor_tensor(out=st.x, in0=centered, scalar=st.vec[:, 1:2], in1=rstd,
                                                        op0=ALU.add, op1=ALU.mult)
                    else:
                        done = dve.tensor_tensor(st.x, centered, rstd, ALU.mult)
                    done.then_inc(s["z"], 1)
                if i < len(steps):
                    st = steps[i]
                    if st.p is not None:
                        dve.wait_ge(s["p"], st.p + 1)
                        pr = bank[st.p % 2]
                        if st.kind == LOAD:
                            done = dve.tensor_copy(st.x, pr[:, 0:COLS])
                        elif st.kind == OUT:
                            done = dve.tensor_copy(st.rows, pr[0:P, 0:CH * D])
                        elif st.kind == LAYER:
                            done = dve.scalar_tensor_tensor(out=st.x, in0=pr[:, 0:COLS], scalar=st.vec[:, 0:1],
                                                            in1=st.x, op0=ALU.max, op1=ALU.add)
                        else:
                            if st.before:
                                dve.wait_ge(s[st.before[0]], st.before[1])
                            done = dve.tensor_tensor(st.x, pr[:, 0:COLS], st.x, ALU.add)
                        done.then_inc(s["first"], 1)
                    elif st.kind == ADD:
                        dve.tensor_tensor(st.x, st.x, st.other, ALU.add).then_inc(s["add"], 1)
        def messages_sync(sp, table_rows):
            for t in range(ETILES):
                now = sums_now[t * ROWS:(t + 1) * ROWS, :].rearrange("(p c) d -> p (c d)", c=CH)
                sp.wait_ge(s["summed"], 2 * t + 2)
                sp.dma_start(table_rows(t), sums[t % 2]).then_inc(s[f"store{t % 2}"], 16)
                sp.dma_start(now, sums[t % 2]).then_inc(s[f"store{t % 2}"], 16)
            messages_stored(sp)

        def messages_stored(eng):
            eng.wait_ge(s["store0"], 32 * ((ETILES + 1) // 2))
            eng.wait_ge(s["store1"], 32 * (ETILES // 2))

        def messages_gpsimd(pool, beside=None):
            for t in range(ETILES):
                if t >= 2:
                    pool.wait_ge(s["sums"], t - 1)
                pool.tensor_copy(same_f[t % 2], same[:, t * CH * P:(t + 1) * CH * P]).then_inc(s["same_f"], 1)
                if beside:
                    beside(t)

        def messages_vector(dve, rels):
            for t in range(ETILES):
                for r in range(rels):
                    k = t * rels + r
                    if k >= 3:
                        dve.wait_ge(s["mm"], k - 2)
                    dve.scalar_tensor_tensor(out=picked[k % 3], in0=kind8[:, t * COLS:(t + 1) * COLS],
                                             scalar=float(r), in1=source_tile(t), op0=ALU.is_equal,
                                             op1=ALU.mult).then_inc(s["picked"], 1)

        def messages_tensor(pe, rels, rel_tile):
            for i in range(ETILES + 2):
                if i < ETILES:
                    if i >= 2:
                        pe.wait_ge(s["sent"], i - 1)
                    for r in range(rels):
                        k = i * rels + r
                        pe.wait_ge(s["picked"], k + 1)
                        pe.matmul(bank[i % 2][:, 0:COLS], rel_tile(r), picked[k % 3], start=(r == 0),
                                  stop=(r == rels - 1)).then_inc(s["mm"], 1)
                if 1 <= i <= ETILES:
                    t = i - 1
                    pe.wait_ge(s["sent"], t + 1)
                    if t >= 2:
                        pe.wait_ge(s["sent_rows"], t - 1)
                    for j in range(PAIRS):
                        last = pe.transpose(bank[2 + t % 2][0:P, j * 128:(j + 1) * 128],
                                            sent[t % 2][:, j * P:(j + 1) * P], ident[:, :])
                    last.then_inc(s["turned"], 1)
                if i >= 2:
                    t = i - 2
                    pe.wait_ge(s["sent_rows"], t + 1)
                    pe.wait_ge(s["same_f"], t + 1)
                    if t >= 2:
                        pe.wait_ge(s["summed"], 2 * t - 2)
                    for c in range(CH):
                        j = c // 2
                        last = pe.matmul(bank[4 + 2 * (t % 2) + c % 2][0:P, j * 128:(j + 1) * 128],
                                         same_f[t % 2][:, c * P:(c + 1) * P],
                                         sent_rows[t % 2][:, j * 128:(j + 1) * 128], start=True, stop=True,
                                         skip_group_check=True)
                    last.then_inc(s["sums"], 1)

        def messages_read(pe):
            for n, times in (("sent", 1), ("sent_rows", 1), ("summed", 2)):
                pe.wait_ge(s[n], times * ETILES)

        def messages_scalar(act, rels):
            for i in range(ETILES + 2):
                if i < ETILES:
                    act.wait_ge(s["mm"], rels * (i + 1))
                    if i >= 2:
                        act.wait_ge(s["turned"], i - 1)
                    act.activation(sent[i % 2], bank[i % 2][:, 0:COLS], ACT.Copy).then_inc(s["sent"], 1)
                if 1 <= i <= ETILES:
                    t = i - 1
                    act.wait_ge(s["turned"], t + 1)
                    if t >= 2:
                        act.wait_ge(s["sums"], t - 1)
                    act.activation(sent_rows[t % 2], bank[2 + t % 2][0:P, :], ACT.Copy).then_inc(s["sent_rows"], 1)
                if i >= 2:
                    t = i - 2
                    act.wait_ge(s["sums"], t + 1)
                    if t >= 2:
                        act.wait_ge(s[f"store{t % 2}"], 32 * (t // 2))
                    for h in range(2):
                        def of_half(a):
                            return a.rearrange("p (j h d) -> p h j d", h=2, d=D)[:, h]
                        act.activation(of_half(sums[t % 2]), of_half(bank[4 + 2 * (t % 2) + h][0:P, :]),
                                       ACT.Copy).then_inc(s["summed"], 1)

        def kind_sync(sp, edge_type, t, stage, ring):
            by_half = edge_type.rearrange("(t j h p) -> h t j p", j=PAIRS, h=2, p=P)
            if t >= ring:
                sp.wait_ge(s["unstaged"], t - ring + 1)
            for h in range(2):
                sp.dma_start(stage[64 * h:64 * h + 64, (t % ring) * COLS:(t % ring + 1) * COLS]
                             .rearrange("q (j p) -> q j p", j=PAIRS),
                             by_half[h, t].partition_broadcast(64)).then_inc(s[f"staged{t % ring}"], 16)

        def kind_vector(dve, t, stage, ring):
            dve.wait_ge(s[f"staged{t % ring}"], 32 * (t // ring + 1))
            dve.tensor_copy(kind8[:, t * COLS:(t + 1) * COLS],
                            stage[:, (t % ring) * COLS:(t % ring + 1) * COLS]).then_inc(s["unstaged"], 1)

        def node_steps(tiles):
            tiles = list(tiles)
            buf = {k: x_buf[i] for i, k in enumerate(tiles)}
            steps = [Step(LOAD, k, buf[k], rows=tile_rows(k % SLOTS)) for k in tiles]
            for l in range(LAYERS):
                steps += [Step(LAYER, k, buf[k], w=w_all[:, l, :], vec=vec[:, l, :]) for k in tiles]
            steps += [Step(SKIP, k, buf[k], rows=tile_rows(k % SLOTS)) for k in tiles]
            steps += [Step(LAST, k, buf[k]) for k in tiles]
            return steps + [Step(OUT, k, buf[k], rows=tile_rows(k % SLOTS)) for k in tiles]

        def mixed(many, few, every):
            steps = []
            for i in range(0, max(len(many), every * len(few)), every):
                steps += many[i:i + every] + few[i // every:i // every + 1]
            return steps

        def node_rows(a, first, k):
            at = first * ROWS + k * ROWS
            part = a[at:at + ROWS, :] if isinstance(at, int) else a[bass.ds(at, ROWS), :]
            return part.rearrange("(p c) d -> p (c d)", c=CH)

        def runs_on_sync(sp):
            for c in range(CH):
                q0 = (c % 4) * ETILES
                sp.dma_start(first_sum[q0:q0 + ETILES, c // 4, :],
                             sums_now[0:EDGES, :].rearrange("(t q) d -> t q d", q=ROWS)[:, c, :]
                             ).then_inc(s["corr_in"], 16)

        def runs_on_gather(pool):
            for h in range(2):
                pool.indirect_dma_start(last_sum[:, h, :], None, sums_now,
                                        bass.IndirectOffsetOnAxis(ap=last_owner_row[:, h:h + 1], axis=0)
                                        ).then_inc(s["corr_got"], 16)

        def runs_on_tensor(pe):
            pe.wait_ge(s["corr_in"], 16 * CH)
            for h in range(2):
                for k in range(2):
                    last = pe.matmul(bank[7][0:Q, h * D:(h + 1) * D], follows[:, k, h, :], first_sum[:, k, :],
                                     start=(h == 0 and k == 0), stop=(h == 1 and k == 1), skip_group_check=True)
            last.then_inc(s["corr"], 1)

        def runs_on_vector(dve, layer):
            dve.wait_ge(s["corr"], 1)
            dve.wait_ge(s["corr_got"], layer * 32 + 32)
            dve.tensor_tensor(last_sum[:, :, :].rearrange("q h d -> q (h d)"), bank[7][0:Q, 0:2 * D],
                              last_sum[:, :, :].rearrange("q h d -> q (h d)"), ALU.add).then_inc(s["corr_sum"], 1)

        def runs_on_scatter(pool, layer):
            pool.wait_ge(s["corr_sum"], 1)
            for to, at in ((sums_now, last_owner_row), (table, last_owner_now)):
                for h in range(2):
                    pool.indirect_dma_start(to, bass.IndirectOffsetOnAxis(ap=at[:, h:h + 1], axis=0),
                                            last_sum[:, h, :], None).then_inc(s["corr_put"], 16)
            pool.wait_ge(s["corr_put"], layer * 64 + 64)
            pool.sem_inc(s["passed"], 1)

        def indices_now(dve):
            dve.tensor_scalar(base[:, :], base[:, :], float(EDGES), None, ALU.add).then_inc(s["now"], 1)
            dve.wait_ge(s["now"], 1)
            dve.tensor_scalar(last_owner_now[:, :], last_owner[:, :], base[0:Q, :], None, ALU.add).then_inc(s["now"], 1)

        def finish_turn():
            nc.all_engine_barrier()
            nc.gpsimd.sem_clear(to_zero)
            nc.all_engine_barrier()

        def small(a, b, n=Q, dt=F32):
            v = work[0:n, a:b]
            return v if dt is F32 else v.bitcast(dt)

        half_chunks = 2 * P
        dst_i, prev_i, src_i = (small(k * half_chunks, (k + 1) * half_chunks, dt=I32) for k in range(3))
        dst_f, prev_f, src_f, own, goal_f, scratch = (small(k * half_chunks, (k + 1) * half_chunks) for k in range(3, 9))
        count = small(2250, 2252)
        last_diag, place_diag = small(2300, 2300 + 2 * Q), small(2500, 2500 + 2 * Q)
        ones = small(2700, 2700 + Q)
        after = small(4000, 4000 + 4 * Q)
        place = small(4400, 4404)
        no_owner = small(4500, 5300, P, I32)
        edge_row = small(6000, 6000 + CHUNKS, P, I32)
        dst_col = small(6200, 6200 + CHUNKS, P)
        zero_row = small(5400, 5400 + D, 1)
        bias_cols = small(5500, 5500 + LAYERS, 128)
        src_col = small(6400, 6400 + CHUNKS, P, U32)
        owner_i = small(6600, 6600 + CHUNKS, P, I32)

        def by_chunk(tile_, k):
            return tile_.rearrange("p (t c) -> p c t", c=CH)[:, 4 * k:4 * k + 4, :]

        with nc.Block() as block:
            @block.sync
            def _(sp):
                n = 0
                dst_t, src_t = (a.rearrange("(t q) -> t q", q=ROWS) for a in (dst, src))
                for c in range(CH):
                    q0, k0 = (c % 4) * ETILES, (c // 4) * P
                    sp.dma_start(dst_i[q0:q0 + ETILES, k0:k0 + P], dst_t[:, c * P:(c + 1) * P]).then_inc(s["rows_in"], 16)
                    sp.dma_start(src_i[q0:q0 + ETILES, k0:k0 + P], src_t[:, c * P:(c + 1) * P]).then_inc(s["rows_in"], 16)
                    if c:
                        sp.dma_start(prev_i[q0:q0 + ETILES, k0:k0 + P],
                                     dst_t[:, c * P - 1:(c + 1) * P - 1]).then_inc(s["rows_in"], 16)
                    n += 3 if c else 2
                sp.dma_start(prev_i[1:ETILES, 0:P], dst[ROWS - 1:EDGES - 1].rearrange("(t q) -> t q", q=ROWS)[:, 0:P]
                             ).then_inc(s["rows_in"], 16)
                sp.dma_start(prev_i[0:1, 1:P], dst[0:P - 1].rearrange("(a n) -> a n", a=1)).then_inc(s["rows_in"], 16)
                sp.dma_start(place, places).then_inc(s["rows_in"], 16)
                assert n + 3 == 26
                sp.wait_ge(s["same_f"], 5)
                for half in range(2):
                    part = slice(64 * half, 64 * half + 64)
                    sp.dma_start(w_all[part, :, part], w_root.rearrange("l d k -> d l k")).then_inc(s["rel"], 16)
                    for dest, a in ((bias_cols[part, :], bias), (vec[part, :, 2], gamma), (vec[part, :, 3], beta)):
                        sp.dma_start(dest, a.rearrange("l d -> d l"), allow_slow_non_contiguous=True).then_inc(s["rel"], 16)
                sp.dma_start(owner_of.rearrange("(p n) o -> p (n o)", p=P), no_owner).then_inc(s["stored"], 16)
                sp.dma_start(sums_now[EDGES:TABLE, :], zero_row).then_inc(s["stored"], 16)
                sp.wait_ge(s["stored"], 32)

            @block.gpsimd
            def _(pool):
                for a in (w_all[:, :, :], rel_now[:, :, :], center[:, :], mean[:, :], ident[:, :]):
                    last = pool.memset(a, 0.0)
                last.then_inc(s["picked"], 1)
                pool.wait_ge(s["picked"], 1)
                for half in range(2):
                    part = slice(64 * half, 64 * half + 64)
                    pool.memset(center[part, part], -1.0 / D)
                    pool.memset(mean[part, part], 1.0 / D).then_inc(s["picked"], 1)
                pool.wait_ge(s["picked"], 3)
                for a, v in ((ident[:, :], 1.0), (center[:, :], 1.0 - 1.0 / D)):
                    pool.affine_select(out=a, in_=a, compare_op=ALU.not_equal, fill=v, base=0,
                                       pattern=[[-1, 128]], channel_multiplier=1).then_inc(s["same_f"], 1)
                pool.memset(eps[:, :], EPS)
                pool.memset(base[:, :], -float(EDGES))
                pool.memset(ones, 1.0).then_inc(s["same_f"], 1)
                pool.memset(no_owner, EDGES).then_inc(s["same_f"], 1)
                pool.iota(edge_row, pattern=[[ROWS, ETILES], [1, CH]], base=0, channel_multiplier=CH)
                pool.memset(zero_row, 0.0).then_inc(s["same_f"], 1)

            @block.vector
            def _(dve):
                done = [0]

                def then(ins):
                    done[0] += 1
                    ins.then_inc(s["z"], 1)
                    dve.wait_ge(s["z"], done[0])

                dve.wait_ge(s["rows_in"], 16 * 26)
                dve.memset(prev_i[0:1, 0:1], -1).then_inc(s["now"], 1)
                dve.wait_ge(s["now"], 1)
                dve.tensor_copy(dst_f, dst_i)
                dve.tensor_copy(src_f, src_i)
                then(dve.tensor_copy(prev_f, prev_i))
                then(dve.tensor_tensor(own, dst_f, prev_f, ALU.not_equal))
                then(dve.tensor_scalar(own, own, -NOWHERE, NOWHERE, ALU.mult, ALU.add))
                then(dve.tensor_tensor(goal_f, own, dst_f, ALU.add))
                for h in range(2):
                    then(dve.tensor_scalar(scratch[:, 0:P], dst_f[:, h * P:(h + 1) * P],
                                           dst_f[:, (h + 1) * P - 1:(h + 1) * P], None, ALU.is_equal, ALU.add,
                                           accum_out=count[:, h:h + 1]))
                then(dve.tensor_scalar(count, count, -float(CH), None, ALU.mult))
                dve.tensor_tensor(last_owner_row[:, :], count, place[:, 2:4], ALU.add)
                then(dve.tensor_tensor(last_owner[:, :], count, place[:, 2:4], ALU.add))
                dve.wait_ge(s["same_f"], 3)
                for h in range(2):
                    dve.tensor_scalar(last_diag[:, h * Q:(h + 1) * Q], ident[0:Q, 0:Q],
                                      dst_f[:, (h + 1) * P - 1:(h + 1) * P], None, ALU.mult)
                    then(dve.tensor_scalar(place_diag[:, h * Q:(h + 1) * Q], ident[0:Q, 0:Q], place[:, h:h + 1],
                                           None, ALU.mult))
                done_before_products = done[0]
                assert done_before_products == 10
                dve.wait_ge(s["p"], 1)
                for k in range(2):
                    psum = [bank[b][0:P, k * Q:(k + 1) * Q].rearrange("p (c t) -> p c t", c=4) for b in range(3)]
                    dve.tensor_copy(by_chunk(dst_col, k), psum[0])
                    dve.tensor_copy(by_chunk(target[:, :], k), psum[0])
                    dve.tensor_copy(by_chunk(goal[:, :], k), psum[1])
                    dve.tensor_copy(by_chunk(src_col, k), psum[2])
                for k in range(2):
                    for h in range(2):
                        a = after[:, (2 * k + h) * Q:(2 * k + h + 1) * Q]
                        then(dve.tensor_scalar(a, bank[4][0:Q, h * Q:(h + 1) * Q], place[:, k:k + 1], None, ALU.is_lt))
                        then(dve.scalar_tensor_tensor(out=follows[:, k, h, :], in0=bank[3][0:Q, h * Q:(h + 1) * Q],
                                                      scalar=dst_f[:, k * P:k * P + 1], in1=a, op0=ALU.is_equal,
                                                      op1=ALU.mult))
                dve.wait_ge(s["rel"], 16 * 8)
                dve.tensor_scalar(vec[:, :, 0], bias_cols, -1.0, None, ALU.mult)
                dve.tensor_copy(center_r[:, :], center[:, :])
                then(dve.tensor_copy(vec[:, :, 1], bank[5][:, 0:LAYERS]))

            @block.tensor
            def _(pe):
                pe.wait_ge(s["z"], 10)
                for k in range(2):
                    for b, a in enumerate((dst_f, goal_f, src_f)):
                        pe.transpose(bank[b][0:P, k * Q:(k + 1) * Q], a[:, k * P:(k + 1) * P], ident[0:Q, 0:Q])
                pe.matmul(bank[3][0:Q, 0:2 * Q], ones, last_diag, start=True, stop=True)
                pe.matmul(bank[4][0:Q, 0:2 * Q], ones, place_diag, start=True, stop=True)
                pe.wait_ge(s["rel"], 16 * 8)
                pe.matmul(bank[5][:, 0:LAYERS], center[:, :], bias_cols, start=True, stop=True).then_inc(s["p"], 1)
        finish_turn()

        with nc.Block() as block:
            dst_here = [source[0:P, i * ROWS:(i + 1) * ROWS].bitcast(I32) for i in range(2)]
            stage = source[:, 2 * ROWS:2 * ROWS + 2 * COLS].bitcast(I32)
            steps = []
            loads = [Step(LOAD, TILES + t, source_tile(t), rows=gathered_rows(t)) for t in reversed(range(ETILES))]
            first = 0
            for g in EARLY_GROUPS:
                group = node_steps(range(first, first + g))
                steps += mixed(group, loads, 3) if first + g == EARLY else group
                first += g
            first_load = next(st for st in steps if st.tile >= TILES)
            number(steps)
            apart = len(steps) // (2 * ETILES + 4)

            @block.sync
            def _(sp):
                def load(k):
                    sp.dma_start(tile_rows(k % SLOTS), node_rows(x, 0, k)).then_inc(s[f"slot{k % SLOTS}"], 16)

                for k in range(SLOTS):
                    load(k)
                for i, st in enumerate(steps):
                    if i % apart == 0 and i // apart < 2 * ETILES:
                        t = i // apart // 2
                        if i // apart % 2:
                            kind_sync(sp, type5, t, stage, 2)
                        else:
                            if t >= 2:
                                sp.wait_ge(s["same_f"], t - 1)
                            sp.dma_start(dst_here[t % 2], dst[t * ROWS:(t + 1) * ROWS].partition_broadcast(P)
                                         ).then_inc(s[f"agg{t % 2}"], 16)
                    if st.kind == OUT:
                        sp.wait_ge(s["first"], st.p + 1)
                        sp.dma_start(node_rows(out, 0, st.tile), st.rows).then_inc(s["stored"], 16)
                        if st.tile + SLOTS < EARLY:
                            sp.wait_ge(s["stored"], 16 * (st.tile + 1))
                            load(st.tile + SLOTS)
                sp.wait_ge(s["first"], steps[-1].p + 1)
                sp.dma_start(source_rows, source[:, :]).then_inc(s["stored"], 16)
                sp.wait_ge(s["stored"], 16 * EARLY + 16)

            @block.gpsimd
            def _(pool):
                for c in range(CHUNKS):
                    pool.indirect_dma_start(gathered[0:P, c * D:(c + 1) * D], None, x,
                                            bass.IndirectOffsetOnAxis(ap=src_col[:, c:c + 1], axis=0)
                                            ).then_inc(s["sources_in"], 16)
                for c in range(CHUNKS):
                    pool.indirect_dma_start(owner_of, bass.IndirectOffsetOnAxis(ap=goal[:, c:c + 1], axis=0),
                                            edge_row[:, c:c + 1], None, bounds_check=NODES - 1,
                                            oob_is_err=False).then_inc(s["owners_put"], 16)
                pool.wait_ge(s["owners_put"], 16 * CHUNKS)
                for c in range(CHUNKS):
                    pool.indirect_dma_start(owner_i[:, c:c + 1], None, owner_of,
                                            bass.IndirectOffsetOnAxis(ap=src_col[:, c:c + 1], axis=0)
                                            ).then_inc(s["owners_got"], 16)
                pool.wait_ge(s["owners_got"], 16 * CHUNKS)

            @block.tensor
            def _(pe):
                def ready(pe, st):
                    if st.kind == LOAD and st.tile < TILES:
                        pe.wait_ge(s[f"slot{st.tile % SLOTS}"], 16 * (st.tile // SLOTS + 1))
                    if st is first_load:
                        pe.wait_ge(s["sources_in"], 16 * CHUNKS)
                stream_tensor(pe, steps, agg_ready=ready)

            @block.scalar
            def _(act):
                act.preload_act_table_set("natural_log_exp_and_others")
                stream_scalar(act, steps)

            @block.vector
            def _(dve):
                def indices(i):
                    f = i // apart - 1
                    if i % apart or not 0 <= f < 2 * ETILES:
                        return
                    t = f // 2
                    if f % 2:
                        kind_vector(dve, t, stage, 2)
                        return
                    dve.wait_ge(s[f"agg{t % 2}"], 16 * (t // 2 + 1))
                    for c in range(CH):
                        k = t * CH + c
                        last = dve.tensor_scalar(same[:, k * P:(k + 1) * P], dst_here[t % 2][:, c * P:(c + 1) * P],
                                                 dst_col[:, k:k + 1], None, ALU.is_equal)
                    last.then_inc(s["same_f"], 1)

                stream_vector(dve, steps, between=indices)
                dve.wait_ge(s["owners_got"], 16 * CHUNKS)
                dve.tensor_copy(owner[:, :], owner_i)
        finish_turn()

        with nc.Fori(0, LAYERS) as turn:
            with nc.Block() as block:
                steps = node_steps(range(NOW))
                sources = [Step(LAYER, TILES + t, source_tile(t), w=w_now[:, :], vec=vec_now[:, :],
                                agg=gathered_rows(t)) for t in range(ETILES)]
                alone = 4 * NOW
                steps = number(steps[:alone] + mixed(steps[alone:], sources, 3))
                first_tile = turn * NOW + EARLY

                @block.sync
                def _(sp):
                    for half in range(2):
                        sp.dma_start(rel_now[64 * half:64 * half + 64, :, 64 * half:64 * half + 64],
                                     w_rel[turn].rearrange("r d k -> d r k")).then_inc(s["rel"], 16)
                    for k in range(NOW):
                        sp.dma_start(tile_rows(k), node_rows(x, first_tile, k)).then_inc(s["rows_in"], 16)
                    messages_sync(sp, lambda t: table[bass.ds(turn * EDGES + t * ROWS, ROWS), :]
                                  .rearrange("(p c) d -> p (c d)", c=CH))
                    runs_on_sync(sp)
                    for st in steps:
                        if st.kind == OUT:
                            sp.wait_ge(s["first"], st.p + 1)
                            sp.dma_start(node_rows(out, first_tile, st.tile), st.rows).then_inc(s["stored"], 16)
                    sp.wait_ge(s["stored"], 16 * NOW)

                @block.gpsimd
                def _(pool):
                    messages_gpsimd(pool)
                    messages_stored(pool)
                    pool.wait_ge(s["now"], 2)
                    runs_on_gather(pool)
                    runs_on_scatter(pool, turn)
                    for c in range(CHUNKS):
                        pool.indirect_dma_start(gathered[0:P, c * D:(c + 1) * D], None, sums_now,
                                                bass.IndirectOffsetOnAxis(ap=owner[:, c:c + 1], axis=0)
                                                ).then_inc(s[f"gathers{c // CH // PORTION}"], 16)

                @block.tensor
                def _(pe):
                    pe.wait_ge(s["rel"], 32)
                    messages_tensor(pe, RELS, lambda r: rel_now[:, r, :])
                    messages_read(pe)
                    pe.wait_ge(s["rows_in"], 16 * NOW)

                    def ready(pe, st):
                        t = st.tile - TILES
                        if t >= 0 and t % PORTION == 0:
                            n = 16 * PORTION * CH
                            pe.wait_ge(s[f"gathers{t // PORTION}"], turn * n + n)
                            pe.wait_ge(s["now2"], 2)
                    stream_tensor(pe, steps, lambda: runs_on_tensor(pe), ready)

                @block.scalar
                def _(act):
                    messages_scalar(act, RELS)
                    act.activation(w_now[:, :], w_all[:, turn, :], ACT.Copy).then_inc(s["now2"], 1)
                    messages_stored(act)
                    act.wait_ge(s["now2"], 2)
                    stream_scalar(act, steps)

                @block.vector
                def _(dve):
                    indices_now(dve)
                    messages_vector(dve, RELS)
                    dve.tensor_copy(vec_now[:, :], vec[:, turn, :]).then_inc(s["now2"], 1)
                    dve.wait_ge(s["now2"], 2)
                    stream_vector(dve, steps, lambda: runs_on_vector(dve, turn))
            finish_turn()

        w1_nat, w1_sb = (rows[:, i * RELS1 * 128:(i + 1) * RELS1 * 128].rearrange("p (r k) -> p r k", r=RELS1)
                         for i in range(2))
        with nc.Block() as block:
            steps = number([Step(ADD, t, source_tile(t), other=gathered[:, t * COLS:(t + 1) * COLS])
                            for t in range(ETILES)])
            stage = work[:, 0:4 * COLS].bitcast(I32)

            @block.sync
            def _(sp):
                for t in range(ETILES):
                    if t % PORTION == 0:
                        part = slice(t * COLS, (t + PORTION) * COLS)
                        sp.dma_start(gathered[:, part], source_rows[:, part]).then_inc(s[f"agg{t // PORTION}"], 16)
                    kind_sync(sp, type16, t, stage, 4)
                sp.wait_ge(s["now"], 1)
                for half in range(2):
                    sp.dma_start(w1_nat[64 * half:64 * half + 64, :, 64 * half:64 * half + 64],
                                 w1.rearrange("r o f -> o r f")).then_inc(s["rel"], 16)

            @block.gpsimd
            def _(pool):
                pool.memset(rows[:, 0:RELS1 * 128], 0.0).then_inc(s["now"], 1)

            @block.tensor
            def _(pe):
                stream_tensor(pe, steps)
                pe.wait_ge(s["rel"], 32)
                pe.wait_ge(s["z"], ETILES)
                for r in range(RELS1):
                    last = pe.transpose(bank[r // 4][:, (r % 4) * 128:(r % 4 + 1) * 128], w1_nat[:, r, :], ident[:, :])
                last.then_inc(s["turned"], 1)

            @block.scalar
            def _(act):
                stream_scalar(act, steps)
                act.wait_ge(s["turned"], 1)
                for b in range(RELS1 // 4):
                    act.activation(w1_sb[:, 4 * b:4 * b + 4, :].rearrange("p r k -> p (r k)"), bank[b][:, :], ACT.Copy)

            @block.vector
            def _(dve):
                def before_step(t):
                    if t < ETILES:
                        kind_vector(dve, t, stage, 4)
                        if t % PORTION == 0:
                            dve.wait_ge(s[f"agg{t // PORTION}"], 16)
                stream_vector(dve, steps, between=before_step)
        finish_turn()

        with nc.Block() as block:
            @block.sync
            def _(sp):
                messages_sync(sp, lambda t: table[LAYERS * EDGES + t * ROWS:LAYERS * EDGES + (t + 1) * ROWS, :]
                              .rearrange("(p c) d -> p (c d)", c=CH))
                runs_on_sync(sp)

            @block.gpsimd
            def _(pool):
                def targets_rows(t):
                    for c in range(t * CH, (t + 1) * CH):
                        pool.indirect_dma_start(gathered[0:P, c * D:(c + 1) * D], None, x,
                                                bass.IndirectOffsetOnAxis(ap=target[:, c:c + 1], axis=0)
                                                ).then_inc(s["targets_in"], 16)
                messages_gpsimd(pool, targets_rows)
                messages_stored(pool)
                pool.wait_ge(s["now"], 2)
                runs_on_gather(pool)
                runs_on_scatter(pool, LAYERS)

            @block.tensor
            def _(pe):
                messages_tensor(pe, RELS1, lambda r: w1_sb[:, r, :])
                messages_read(pe)
                runs_on_tensor(pe)

            @block.scalar
            def _(act):
                messages_scalar(act, RELS1)

            @block.vector
            def _(dve):
                indices_now(dve)
                messages_vector(dve, RELS1)
                runs_on_vector(dve, LAYERS)
        finish_turn()

        ring = 5
        agg_buf = [work[0:P, i * CH * D:(i + 1) * CH * D] for i in range(ring)]
        with nc.Block() as block:
            steps, tail, first = [], [], 0
            for g in TARGET_GROUPS:
                tiles = range(first, first + g)
                first += g
                group = [Step(LOAD, t, source_tile(t), rows=gathered_rows(t)) for t in tiles]
                for l in range(LAYERS):
                    group += [Step(LAYER, t, source_tile(t), w=w_all[:, l, :], vec=vec[:, l, :], agg=True, layer=l)
                              for t in tiles]
                steps += mixed(group, tail, 2)
                tail = [Step(SKIP, t, source_tile(t), rows=gathered_rows(t)) for t in tiles]
                tail += [Step(LAST, t, source_tile(t), rows=True, layer=LAYERS) for t in tiles]
                tail += [Step(OUT, t, source_tile(t), rows=gathered_rows(t)) for t in tiles]
            steps = number(steps + tail)
            with_agg = [st for st in steps if st.kind in (LAYER, LAST)]
            for i, st in enumerate(with_agg):
                st.order = i
                if st.kind == LAYER:
                    st.agg = agg_buf[i % ring]
                else:
                    st.rows = agg_buf[i % ring]

            @block.sync
            def _(sp):
                for i, st in enumerate(with_agg):
                    if i >= ring:
                        sp.wait_ge(s["p"], with_agg[i - ring].p + 1)
                    at = st.layer * EDGES + st.tile * ROWS
                    sp.dma_start(agg_buf[i % ring], table[at:at + ROWS, :].rearrange("(p c) d -> p (c d)", c=CH)
                                 ).then_inc(s[f"agg{i % ring}"], 16)

            @block.gpsimd
            def _(pool):
                for st in steps:
                    if st.kind == OUT:
                        pool.wait_ge(s["first"], st.p + 1)
                        for c in range(CH):
                            at = st.tile * CH + c
                            pool.indirect_dma_start(out, bass.IndirectOffsetOnAxis(ap=goal[:, at:at + 1], axis=0),
                                                    st.rows[:, c * D:(c + 1) * D], None, bounds_check=NODES - 1,
                                                    oob_is_err=False).then_inc(s["put"], 16)
                pool.wait_ge(s["put"], 16 * CHUNKS)

            @block.tensor
            def _(pe):
                pe.wait_ge(s["targets_in"], 16 * CHUNKS)

                def ready(pe, st):
                    if st.kind in (LAYER, LAST):
                        pe.wait_ge(s[f"agg{st.order % ring}"], 16 * (st.order // ring + 1))
                stream_tensor(pe, steps, agg_ready=ready)

            @block.scalar
            def _(act):
                stream_scalar(act, steps)

            @block.vector
            def _(dve):
                stream_vector(dve, steps)


def kernel(**inputs):
    import concourse.bacc as _bacc
    from concourse.bass_utils import run_bass_kernel_spmd as _run

    names = ["x", "src", "dst", "edge_type_16", "edge_type_5", "L0_gnn_W_rel", "L0_gnn_W_root", "L0_gnn_bias",
             "L0_gnn_ln_gamma", "L0_gnn_ln_beta", "L1_gnn_W"]
    t, c = np.divmod(np.arange(CHUNKS), CH)
    places = np.zeros((Q, 4), np.float32)
    places[(c % 4) * ETILES + t, c // 4] = t * CH + c
    places[(c % 4) * ETILES + t, 2 + c // 4] = t * ROWS + c + ROWS
    nc = _bacc.Bacc("TRN2", target_bir_lowering=False, num_devices=1)
    arrays, args = {}, []
    for name in names:
        arrays["in_" + name] = np.ascontiguousarray(inputs[name])
    arrays["in_places"] = places
    for name, a in arrays.items():
        args.append(nc.dram_tensor(name, a.shape, mybir.dt.from_np(a.dtype), kind="ExternalInput").ap())
    args.append(nc.dram_tensor("out_0", (NODES, D), F32, kind="ExternalOutput").ap())
    build(nc, *args)
    r = _run(nc, [arrays], core_ids=[0])
    return r.results[0]["out_0"]
```
